# Optimizing a Trainium2 kernel written in Bass

```python
import numpy as np
import jax
import jax.numpy as jnp

def _softmax(x, axis=-1):
    return jax.nn.softmax(x, axis=axis)

def _gelu(x):
    return jax.nn.gelu(x, approximate=True)

def _silu(x):
    return jax.nn.silu(x)

def _sigmoid(x):
    return jax.nn.sigmoid(x)

def _layernorm(x, axis=-1, eps=1e-05):
    m = jnp.mean(x, axis=axis, keepdims=True)
    v = jnp.var(x, axis=axis, keepdims=True)
    return (x - m) / jnp.sqrt(v + eps)

def _scatter_add(tgt, idx, src, axis=0):
    return tgt.at[idx].add(src)

def _segment_sum(src, seg, n):
    return jax.ops.segment_sum(src, seg, n)
kernel_name = 'mk_gnn_preln_d1_gnn_r64_c80b62'

def setup_inputs(seed: int=0):
    np.random.seed(seed)
    _w = jnp.asarray

    def _rec_inputs():
        import jax
        import jax.numpy as jnp
        _gk = jax.random.key(seed)
        x = -0.0008691 + 1 * jax.random.normal(jax.random.fold_in(_gk, 1), (50000, 128), jnp.float32)
        src = jax.random.randint(jax.random.fold_in(_gk, 2), (12500,), 0, 50000, jnp.int32)
        dst = jax.random.randint(jax.random.fold_in(_gk, 3), (12500,), 0, 50000, jnp.int32)
        _o = jnp.argsort(dst, stable=True)
        src = src[_o]
        dst = dst[_o]
        edge_attr_3 = 0.000463381 + 0.999898 * jax.random.normal(jax.random.fold_in(_gk, 12), (12500, 3), jnp.float32)
        edge_attr_32 = jax.random.uniform(jax.random.fold_in(_gk, 13), (12500, 32), jnp.float32, 0.0, 1)
        edge_attr_5 = 0.000898722 + 1.00012 * jax.random.normal(jax.random.fold_in(_gk, 14), (12500, 5), jnp.float32)
        return (x, src, dst, edge_attr_3, edge_attr_32, edge_attr_5)
    x, src, dst, edge_attr_3, edge_attr_32, edge_attr_5 = _rec_inputs()

    def _L0_gnn_setup():
        import jax, jax.numpy as jnp
        import numpy as np
        N_ATOMS, N_PAIRS, F_DIM, N_RBF = (10000, 4000, 128, 32)
        N_MLPS = 5

        def _silu(x):
            return x * jax.nn.sigmoid(x)

        def _resmlp(x, w1, b1, w2, b2, wout):
            h = x + jnp.dot(_silu(jnp.dot(_silu(x), w1) + b1), w2) + b2
            return jnp.dot(_silu(h), wout)
        key = jax.random.key(seed)
        ks = jax.random.split(key, 16)
        f_scale = F_DIM ** (-0.5)
        r_scale = N_RBF ** (-0.5)
        return {'x': jax.random.normal(ks[0], (N_ATOMS, F_DIM), dtype=jnp.float32), 'rbf': jax.random.uniform(ks[1], (N_PAIRS, N_RBF), dtype=jnp.float32), 'pij': jax.random.normal(ks[2], (N_PAIRS, 3), dtype=jnp.float32), 'dij': jax.random.normal(ks[3], (N_PAIRS, 5), dtype=jnp.float32), 'w_rs': jax.random.normal(ks[4], (N_RBF, F_DIM), dtype=jnp.float32) * r_scale, 'w_rp': jax.random.normal(ks[5], (N_RBF, F_DIM), dtype=jnp.float32) * r_scale, 'w_rd': jax.random.normal(ks[6], (N_RBF, F_DIM), dtype=jnp.float32) * r_scale, 'w_pp': jax.random.normal(ks[7], (F_DIM, 2 * F_DIM), dtype=jnp.float32) * f_scale, 'w_pd': jax.random.normal(ks[8], (F_DIM, 2 * F_DIM), dtype=jnp.float32) * f_scale, 'res_w1': jax.random.normal(ks[9], (N_MLPS, F_DIM, F_DIM), dtype=jnp.float32) * f_scale, 'res_b1': jnp.zeros((N_MLPS, F_DIM), dtype=jnp.float32), 'res_w2': jax.random.normal(ks[10], (N_MLPS, F_DIM, F_DIM), dtype=jnp.float32) * f_scale, 'res_b2': jnp.zeros((N_MLPS, F_DIM), dtype=jnp.float32), 'res_wout': jax.random.normal(ks[11], (N_MLPS, F_DIM, F_DIM), dtype=jnp.float32) * f_scale, 'idx_i': jnp.sort(jax.random.randint(ks[12], (N_PAIRS,), 0, N_ATOMS, dtype=jnp.int32)), 'idx_j': jax.random.randint(ks[13], (N_PAIRS,), 0, N_ATOMS, dtype=jnp.int32)}
    _L0_gnn_all = _L0_gnn_setup()
    _L0_gnn_in = {k: v for k, v in _L0_gnn_all.items() if k in ('w_rs', 'w_rp', 'w_rd', 'w_pp', 'w_pd', 'res_w1', 'res_b1', 'res_w2', 'res_b2', 'res_wout')}
    del _L0_gnn_all
    return {'x': x, 'src': src, 'dst': dst, 'edge_attr_3': edge_attr_3, 'edge_attr_32': edge_attr_32, 'edge_attr_5': edge_attr_5, 'L0_gnn_w_rs': _L0_gnn_in['w_rs'], 'L0_gnn_w_rp': _L0_gnn_in['w_rp'], 'L0_gnn_w_rd': _L0_gnn_in['w_rd'], 'L0_gnn_w_pp': _L0_gnn_in['w_pp'], 'L0_gnn_w_pd': _L0_gnn_in['w_pd'], 'L0_gnn_res_w1': _L0_gnn_in['res_w1'], 'L0_gnn_res_b1': _L0_gnn_in['res_b1'], 'L0_gnn_res_w2': _L0_gnn_in['res_w2'], 'L0_gnn_res_b2': _L0_gnn_in['res_b2'], 'L0_gnn_res_wout': _L0_gnn_in['res_wout']}

def reference(x, src, dst, edge_attr_3, edge_attr_32, edge_attr_5, L0_gnn_w_rs, L0_gnn_w_rp, L0_gnn_w_rd, L0_gnn_w_pp, L0_gnn_w_pd, L0_gnn_res_w1, L0_gnn_res_b1, L0_gnn_res_w2, L0_gnn_res_b2, L0_gnn_res_wout):
    import jax
    import jax.numpy as jnp

    def _L0_gnn_ref(x, rbf, pij, dij, w_rs, w_rp, w_rd, w_pp, w_pd, res_w1, res_b1, res_w2, res_b2, res_wout, idx_i, idx_j):
        import jax, jax.numpy as jnp
        import numpy as np
        N_ATOMS, N_PAIRS, F_DIM, N_RBF = (10000, 4000, 128, 32)
        N_MLPS = 5

        def _silu(x):
            return x * jax.nn.sigmoid(x)

        def _resmlp(x, w1, b1, w2, b2, wout):
            h = x + jnp.dot(_silu(jnp.dot(_silu(x), w1) + b1), w2) + b2
            return jnp.dot(_silu(h), wout)
        n = x.shape[0]
        gs = jnp.dot(rbf, w_rs)
        gp = jnp.dot(rbf, w_rp)[:, None, :] * pij[:, :, None]
        gd = jnp.dot(rbf, w_rd)[:, None, :] * dij[:, :, None]
        xx = _resmlp(x, res_w1[0], res_b1[0], res_w2[0], res_b2[0], res_wout[0])
        xs = _resmlp(x, res_w1[1], res_b1[1], res_w2[1], res_b2[1], res_wout[1])[idx_j]
        xp = _resmlp(x, res_w1[2], res_b1[2], res_w2[2], res_b2[2], res_wout[2])[idx_j]
        xd = _resmlp(x, res_w1[3], res_b1[3], res_w2[3], res_b2[3], res_wout[3])[idx_j]
        s = xx + jax.ops.segment_sum(gs * xs, idx_i, num_segments=n)
        p = jax.ops.segment_sum(gp * xp[:, None, :], idx_i, num_segments=n)
        d = jax.ops.segment_sum(gd * xd[:, None, :], idx_i, num_segments=n)
        pa, pb = jnp.split(jnp.dot(p, w_pp), 2, axis=-1)
        da, db = jnp.split(jnp.dot(d, w_pd), 2, axis=-1)
        y = s + (pa * pb).sum(-2) + (da * db).sum(-2)
        return _resmlp(y, res_w1[4], res_b1[4], res_w2[4], res_b2[4], res_wout[4])
    h = jnp.maximum(_layernorm(x, axis=-1), 0.0)
    x = x + _L0_gnn_ref(h, edge_attr_32, edge_attr_3, edge_attr_5, L0_gnn_w_rs, L0_gnn_w_rp, L0_gnn_w_rd, L0_gnn_w_pp, L0_gnn_w_pd, L0_gnn_res_w1, L0_gnn_res_b1, L0_gnn_res_w2, L0_gnn_res_b2, L0_gnn_res_wout, src, dst)
    return x

_drawn_inputs = setup_inputs


def setup_inputs(seed=0):
    import zlib

    import numpy as np

    out = dict(_drawn_inputs(seed))
    spreads = {'L0_gnn_res_b1': (0.0, 0.1), 'L0_gnn_res_b2': (0.0, 0.1)}
    factors = {}
    for name, (base, spread) in spreads.items():
        noise = np.random.default_rng([zlib.crc32(name.encode()), seed]).standard_normal(out[name].shape)
        drawn = base * np.exp(spread * noise) if base else spread * noise
        out[name] = jnp.asarray(drawn.astype(out[name].dtype))
    for name, factor in factors.items():
        out[name] = (out[name] * factor).astype(out[name].dtype)
    return out
```

```python
import concourse.bass as bass
from concourse import mybir
from contextlib import ExitStack


class Step:

    def __init__(self, i, c, unroll, total):
        self.i, self.c, self.unroll, self.total = i, c, unroll, total
        self.peeled = isinstance(i, int)

    def live(self, lag=0):
        return not self.peeled or 0 <= self.c - lag < self.total

    def has(self, lag):
        return not self.peeled or self.c - lag >= 0

    def n(self, lag=0):
        return self.i * self.unroll + (self.c - lag)

    def slot(self, lag=0):
        return (self.c - lag) % self.unroll

    def uses(self, lag=0):
        return self.i + (self.c - lag) // self.unroll + 1


def alone(eng, passed):
    eng.sem_inc(passed, 1)


def run_steps(eng, body, unroll, total, first, last_lag, ahead):
    begin = -(-first // unroll)
    end = (total - ahead) // unroll
    if end - begin < 2:
        begin = end = 0
    for c in range(begin * unroll):
        body(Step(0, c, unroll, total))
    if end > begin:
        with eng.Fori(begin, end) as i:
            for c in range(unroll):
                body(Step(i, c, unroll, total))
    for c in range(end * unroll, total + last_lag):
        body(Step(0, c, unroll, total))


def gnn_kernel(nc, x, src, dst, attr3, attr32, attr5, w_rs, w_rp, w_rd, w_pp, w_pd,
               w1, b1, w2, b2, wout, out):
    fp32, i32, bf16 = mybir.dt.float32, mybir.dt.int32, mybir.dt.bfloat16
    ALU = mybir.AluOpType
    ACT = mybir.ActivationFunctionType
    AX = mybir.AxisListType

    P = 128
    N, F = x.shape
    E = src.shape[0]
    NRBF, NP3, ND5, NMLP = attr32.shape[1], attr3.shape[1], attr5.shape[1], w1.shape[0]
    EPS = 1e-5

    TB = 4
    BLOCK = TB * P
    NB = -(-N // BLOCK)

    T = -(-E // P)
    T += T % 2
    FULL_P = E // T
    REST = E - FULL_P * T

    V = 5
    R = P - V
    G = -(-(-(-E // R)) // TB)
    ROWS = G * TB * R
    C_ONE, C_P, C_D, C_RBF = 0, V, 2 * V, 3 * V
    KT = 3 * V + NRBF
    W = 2 + KT
    PAD = N
    LOW = 256

    xb_view = lambda row, dram: dram[row, :].rearrange("(p t) f -> p t f", t=TB)

    ctx = ExitStack()
    with ctx:
        def sb(name, shape, dt=fp32):
            return ctx.enter_context(nc.sbuf_tensor(name, shape, dt))

        def sem(name):
            return ctx.enter_context(nc.semaphore(name))

        by_low = nc.dram_tensor("edges_by_low", [P * T, W], fp32, kind="Internal").ap()
        by_src = nc.dram_tensor("edges_by_src", [ROWS + 2, W], fp32, kind="Internal").ap()
        ysum = nc.dram_tensor("node_sums", [N + P, F], fp32, kind="Internal").ap()

        ident = sb("ident", [P, P])
        ident_h = sb("ident_h", [P, P], bf16)
        before_h = sb("before_h", [P, P], bf16)
        ones_h = sb("ones_h", [P, P], bf16)
        digits_h = sb("digits_h", [P, LOW], bf16)
        column = sb("column", [P, LOW])
        part = sb("part", [P, 1])
        trash = sb("trash", [P, 1])
        is_real = sb("is_real", [P, 1])
        mask_p = sb("mask_p", [P, 1])
        mask_d = sb("mask_d", [P, 1])
        ge = sb("ge", [P, 4])
        neghalf = sb("neghalf", [P, TB])
        unit = sb("unit", [V, TB, 3 * V])
        w1_sb = sb("w1_sb", [P, NMLP, F])
        w2_sb = sb("w2_sb", [P, NMLP, F])
        wo_sb = sb("wo_sb", [P, NMLP, F])
        b1_sb = sb("b1_sb", [P, NMLP])
        b2_sb = sb("b2_sb", [P, NMLP])
        wr_sb = sb("wr_sb", [KT, 3, F])
        wpp_sb = sb("wpp_sb", [P, 2 * F])
        wpd_sb = sb("wpd_sb", [P, 2 * F])
        zeros = sb("zeros", [P, 4 * F])

        psum = [ctx.enter_context(nc.psum_tensor(f"bank{i}", [P, 512], fp32)) for i in range(8)]

        with ExitStack() as own:
            def psb(name, shape, dt=fp32):
                return own.enter_context(nc.sbuf_tensor(name, shape, dt))

            def psem(name):
                return own.enter_context(nc.semaphore(name))

            pay = psb("pay", [P, T, W])
            st_src = psb("st_src", [P, T], i32)
            st_dst = psb("st_dst", [P, T], i32)
            st3 = psb("st3", [P, T, NP3])
            st5 = psb("st5", [P, T, ND5])
            st32 = psb("st32", [P, T, NRBF])
            digit_i = psb("digit_i", [P, T], i32)
            digit_f = psb("digit_f", [P, T])
            onehot = psb("onehot", [P, T, LOW], bf16)
            total = psb("total", [P, LOW])
            upto = psb("upto", [P, LOW])
            base = psb("base", [P, LOW])
            picked = psb("picked", [P, 2, LOW])
            rank_f = psb("rank_f", [P, T])
            rank_i = psb("rank_i", [P, T], i32)
            padrow = psb("padrow", [P, 3, W])
            leadrow = psb("leadrow", [1, W])

            s_w = psem("weights_in")
            s_cst = psem("constants_made")
            s_dc = psem("dve_constants")
            s_staged = psem("stages_cleared")
            s_edges = psem("edges_in")
            s_pay = psem("payload_made")
            s_init = psem("tables_initialised")
            s_dig = psem("digits_made")
            s_oh = psem("onehots_made")
            s_cnt = psem("counts_done")
            s_dve = psem("dve_chain")
            s_base = psem("bases_made")
            s_seed = psem("bases_added")
            s_pick = psem("ranks_picked")
            s_add = psem("tiles_added")
            s_sum = psem("ranks_summed")
            s_rank = psem("rank_indices_made")
            s_scat = [psem("scattered_by_low"), psem("scattered_by_src")]
            s_back = psem("sorted_by_low_in")

            PREP_LOADS = 11
            pads = ROWS + 1 - P * T
            groups = []
            at = P * T + 1
            left = pads
            while left:
                each = 3 if left >= 3 else 1
                parts = min(P, left // each)
                groups.append((at, parts, each))
                at += parts * each
                left -= parts * each

            def parts_of(dram, tile, eng, s, per):
                n = 0
                cut = FULL_P // 16 * 16
                flat = dram.rearrange("e c -> (e c)") if per > 1 or len(dram.shape) == 2 else dram
                for lo, hi in ((0, cut), (cut, FULL_P)):
                    if hi > lo:
                        eng.dma_start(tile[lo:hi, :], flat[lo * T * per:hi * T * per].rearrange("(p c) -> p c", p=hi - lo)).then_inc(s, 16)
                        n += 1
                if REST:
                    eng.dma_start(tile[FULL_P:FULL_P + 1, 0:REST * per], flat[FULL_P * T * per:E * per].rearrange("(p c) -> p c", p=1)).then_inc(s, 16)
                    n += 1
                return n

            NE = (1 if FULL_P >= 16 else 0) + (1 if FULL_P % 16 else 0) + (1 if REST else 0)

            with nc.Block() as block:
                @block.sync
                def _(sp):
                    sp.wait_ge(s_staged, 1)
                    parts_of(src, st_src[:, :], sp, s_edges, 1)
                    parts_of(dst, st_dst[:, :], sp, s_edges, 1)
                    parts_of(attr3, st3[:, :, :].rearrange("p t c -> p (t c)"), sp, s_edges, NP3)
                    parts_of(attr5, st5[:, :, :].rearrange("p t c -> p (t c)"), sp, s_edges, ND5)
                    parts_of(attr32, st32[:, :, :].rearrange("p t c -> p (t c)"), sp, s_edges, NRBF)
                    sp.dma_start(w1_sb[:, :, :], w1.rearrange("m k n -> k m n")).then_inc(s_w, 16)
                    sp.dma_start(w2_sb[:, :, :], w2.rearrange("m k n -> k m n")).then_inc(s_w, 16)
                    sp.dma_start(wo_sb[:, :, :], wout.rearrange("m k n -> k m n")).then_inc(s_w, 16)
                    for m in range(NMLP):
                        sp.dma_start(b1_sb[:, m:m + 1], b1[m:m + 1, :].rearrange("o k -> k o")).then_inc(s_w, 16)
                        sp.dma_start(b2_sb[:, m:m + 1], b2[m:m + 1, :].rearrange("o k -> k o")).then_inc(s_w, 16)
                    sp.dma_start(wr_sb[C_RBF:KT, 0, :], w_rp).then_inc(s_w, 16)
                    sp.dma_start(wr_sb[C_RBF:KT, 1, :], w_rd).then_inc(s_w, 16)
                    sp.dma_start(wr_sb[C_RBF:KT, 2, :], w_rs).then_inc(s_w, 16)
                    sp.dma_start(wpp_sb[:, :], w_pp).then_inc(s_w, 16)
                    sp.dma_start(wpd_sb[:, :], w_pd).then_inc(s_w, 16)
                    sp.dma_start(by_src[0:1, :], leadrow[:, :]).then_inc(s_init, 16)
                    for row, parts, each in groups:
                        sp.dma_start(by_src[row:row + parts * each, :].rearrange("(p t) w -> p t w", t=each),
                                     padrow[0:parts, 0:each, :]).then_inc(s_init, 16)
                    sp.dma_start(ysum[N:N + P, :], zeros[:, 0:F]).then_inc(s_init, 16)
                    sp.wait_ge(s_scat[0], 16 * T)
                    sp.dma_start(pay[:, :, :], by_low.rearrange("(p t) w -> p t w", t=T)).then_inc(s_back, 16)
                    sp.wait_ge(s_w, 16 * (8 + 2 * NMLP))
                    sp.wait_ge(s_init, 16 * (2 + len(groups)))

                @block.gpsimd
                def _(pool):
                    nc.gpsimd.memset(st_src[:, :], PAD)
                    nc.gpsimd.memset(st_dst[:, :], 0)
                    nc.gpsimd.memset(st3[:, :, :], 0.0)
                    nc.gpsimd.memset(st5[:, :, :], 0.0)
                    nc.gpsimd.memset(st32[:, :, :], 0.0)
                    nc.gpsimd.memset(zeros[:, :], 0.0)
                    nc.gpsimd.memset(padrow[:, :, :], 0.0)
                    nc.gpsimd.memset(leadrow[:, :], 0.0)
                    nc.gpsimd.memset(wr_sb[:, :, :], 0.0).then_inc(s_cst, 1)
                    pool.wait_ge(s_cst, 1)
                    nc.gpsimd.memset(padrow[:, :, 0:1].bitcast(i32), PAD)
                    nc.gpsimd.memset(leadrow[:, 0:1].bitcast(i32), PAD + 1).then_inc(s_staged, 1)
                    nc.gpsimd.iota(column[:, :], [[1, LOW]], base=0, channel_multiplier=0,
                                   allow_small_or_imprecise_dtypes=True)
                    nc.gpsimd.iota(part[:, :], [[0, 1]], base=0, channel_multiplier=1,
                                   allow_small_or_imprecise_dtypes=True)
                    nc.gpsimd.memset(neghalf[:, :], -0.5)
                    nc.gpsimd.memset(ones_h[:, :], 1.0)
                    nc.gpsimd.memset(pay[:, :, :], 0.0).then_inc(s_cst, 1)
                    for n in range(2):
                        pool.wait_ge(s_rank, n + 1)
                        if n == 0:
                            pool.wait_ge(s_pay, 1)
                        else:
                            pool.wait_ge(s_init, 16 * (2 + len(groups)))
                        for t in range(T):
                            nc.gpsimd.indirect_dma_start(
                                out=(by_low, by_src)[n], out_offset=bass.IndirectOffsetOnAxis(ap=rank_i[:, t:t + 1], axis=0),
                                in_=pay[:, t, :], in_offset=None).then_inc(s_scat[n], 16)
                        if n == 0:
                            pool.wait_ge(s_scat[0], 16 * T)
                    pool.wait_ge(s_scat[1], 16 * T)

                @block.scalar
                def _(act):
                    act.wait_ge(s_cst, 2)
                    act.wait_ge(s_edges, 16 * 5 * NE)
                    nc.scalar.copy(pay[:, :, 2 + C_P:2 + C_P + NP3], st3[:, :, :])
                    nc.scalar.copy(pay[:, :, 2 + C_D:2 + C_D + ND5], st5[:, :, :])
                    nc.scalar.copy(pay[:, :, 2 + C_RBF:2 + C_RBF + NRBF], st32[:, :, :]).then_inc(s_pay, 1)

                @block.vector
                def _(dve):
                    n_chain = [0]

                    def link(ins):
                        n_chain[0] += 1
                        ins.then_inc(s_dve, 1)
                        dve.wait_ge(s_dve, n_chain[0])

                    dve.wait_ge(s_cst, 2)
                    dve.sem_inc(s_sum, 1)
                    nc.vector.tensor_copy(digits_h[:, :], column[:, :])
                    nc.vector.tensor_scalar(ident[:, :], column[:, 0:P], part[:, 0:1], None, ALU.is_equal)
                    nc.vector.tensor_scalar(ident_h[:, :], column[:, 0:P], part[:, 0:1], None, ALU.is_equal)
                    nc.vector.tensor_scalar(before_h[:, :], column[:, 0:P], part[:, 0:1], None, ALU.is_gt)
                    nc.vector.tensor_scalar(trash[:, :], part[:, :], float(N), None, ALU.add)
                    nc.vector.tensor_scalar(is_real[:, :], part[:, :], float(V), None, ALU.is_ge)
                    for n in range(3):
                        nc.vector.tensor_scalar(ge[:, n:n + 1], part[:, :], float((n + 1) * V), None, ALU.is_ge)
                    link(nc.vector.memset(pay[:, :, 2:3], 1.0))
                    nc.vector.tensor_tensor(mask_p[:, :], ge[:, 0:1], ge[:, 1:2], ALU.subtract)
                    nc.vector.tensor_tensor(mask_d[:, :], ge[:, 1:2], ge[:, 2:3], ALU.subtract)
                    link(nc.vector.memset(unit[:, :, :], 0.0))
                    for t in range(TB):
                        nc.vector.memset(unit[:, t, 0:1], 1.0)
                        nc.vector.tensor_copy(unit[:, t, V:V + NP3], ident[0:V, 0:NP3])
                        last = nc.vector.tensor_copy(unit[:, t, 2 * V:2 * V + ND5], ident[0:V, 0:ND5])
                    last.then_inc(s_dc, 1)
                    dve.wait_ge(s_edges, 16 * 5 * NE)
                    nc.vector.tensor_copy(pay[:, :, 0:1].bitcast(i32), st_src[:, :].unsqueeze(2))
                    link(nc.vector.tensor_copy(pay[:, :, 1:2].bitcast(i32), st_dst[:, :].unsqueeze(2)))
                    for n in range(2):
                        key = pay[:, :, 0].bitcast(i32)
                        if n == 0:
                            link(nc.vector.tensor_single_scalar(digit_i[:, :], key, LOW - 1, op=ALU.bitwise_and))
                        else:
                            dve.wait_ge(s_back, 16)
                            link(nc.vector.tensor_single_scalar(digit_i[:, :], key, LOW.bit_length() - 1, op=ALU.arith_shift_right))
                        link(nc.vector.tensor_copy(digit_f[:, :], digit_i[:, :]))
                        if n == 1:
                            dve.wait_ge(s_add, T)
                        with dve.Fori(0, T) as t:
                            nc.vector.tensor_scalar(onehot[:, t, :], digits_h[:, :], digit_f[:, bass.ds(t, 1)], None,
                                                    ALU.is_equal).then_inc(s_oh, 1)
                        dve.wait_ge(s_cnt, n + 1)
                        link(nc.vector.tensor_copy(total[:, :], psum[2][:, 0:LOW]))
                        link(nc.vector.tensor_tensor_scan(upto[:, :], total[:, :], zeros[:, 0:LOW], 0.0, ALU.add, ALU.add))
                        nc.vector.tensor_tensor(base[:, :], upto[:, :], total[:, :], ALU.subtract).then_inc(s_base, 1)
                        with dve.Fori(0, T // 2) as i:
                            dve.wait_ge(s_sum, i + (1 + n * T // 2))
                            for c in range(2):
                                dve.wait_ge(s_seed, i * 2 + (c + 1 + n * T))
                                nc.vector.tensor_tensor(picked[:, c, :], psum[c][:, 0:LOW], onehot[:, i * 2 + c, :],
                                                        ALU.mult).then_inc(s_pick, 1)
                            dve.wait_ge(s_pick, i * 2 + (2 + n * T))
                            nc.vector.tensor_reduce(rank_f[:, bass.ds(i * 2, 2)], picked[:, :, :], AX.X, ALU.add).then_inc(s_sum, 1)
                        dve.wait_ge(s_sum, 1 + (n + 1) * T // 2)
                        dve.wait_ge(s_pick, (n + 1) * T)
                        nc.vector.tensor_scalar(rank_i[:, :], rank_f[:, :], float(n), None, ALU.add).then_inc(s_rank, 1)
                        if n == 0:
                            dve.wait_ge(s_scat[0], 16 * T)
                    dve.wait_ge(s_dc, 1)

                @block.tensor
                def _(pe):
                    pe.wait_ge(s_dc, 1)
                    pe.wait_ge(s_cst, 2)
                    for n in range(2):
                        if n == 1:
                            pe.wait_ge(s_pick, T)
                            pe.wait_ge(s_base, 1)
                        def count(t, start):
                            nc.tensor.matmul(psum[0][:, 0:LOW], before_h[:, :], onehot[:, t, :], start=start, stop=True, skip_group_check=True)
                            nc.tensor.matmul(psum[1][:, 0:LOW], before_h[:, :], onehot[:, t, :], start=start, stop=True, skip_group_check=True)
                            return nc.tensor.matmul(psum[2][:, 0:LOW], ones_h[:, :], onehot[:, t, :], start=start, stop=True, skip_group_check=True)
                        pe.wait_ge(s_oh, n * T + 1)
                        count(0, True)
                        with pe.Fori(1, T - 1) as t:
                            pe.wait_ge(s_oh, t + (n * T + 1))
                            count(t, False)
                        pe.wait_ge(s_oh, n * T + T)
                        count(T - 1, False).then_inc(s_cnt, 1)
                        pe.wait_ge(s_base, n + 1)
                        nc.tensor.matmul(psum[0][:, 0:LOW], ident[:, :], base[:, :], start=False, stop=True, skip_group_check=True).then_inc(s_seed, 1)
                        nc.tensor.matmul(psum[1][:, 0:LOW], ident[:, :], base[:, :], start=False, stop=True, skip_group_check=True)
                        nc.tensor.matmul(psum[1][:, 0:LOW], ident_h[:, :], onehot[:, 0, :], start=False, stop=True, skip_group_check=True).then_inc(s_seed, 1)
                        def advance(i, c):
                            pe.wait_ge(s_pick, i * 2 + (c + 1 + n * T))
                            nc.tensor.matmul(psum[c][:, 0:LOW], ident_h[:, :], onehot[:, i * 2 + c, :], start=False, stop=True, skip_group_check=True)
                            return nc.tensor.matmul(psum[c][:, 0:LOW], ident_h[:, :], onehot[:, i * 2 + (c + 1), :], start=False, stop=True, skip_group_check=True)
                        with pe.Fori(0, T // 2 - 1) as i:
                            for c in range(2):
                                advance(i, c).then_inc(s_seed, 1)
                        pe.wait_ge(s_pick, (n + 1) * T)
                        pe.sem_inc(s_add, T)

        xin = sb("xin", [P, 4, TB, F])
        yin = sb("yin", [P, 4, TB, F])
        xn = sb("xn", [P, 4, TB, F])
        stats = sb("stats", [P, 4, TB, 6])
        mv = sb("mv", [P, 4, TB, 2])
        ve = sb("ve", [P, 4, TB])
        rstd = sb("rstd", [P, 4, TB])
        hT = sb("hT", [P, 4, BLOCK])
        s1 = sb("s1", [P, 4, BLOCK])
        s2 = sb("s2", [P, 4, BLOCK])
        h2 = sb("h2", [P, 4, BLOCK])
        s3 = sb("s3", [P, 4, BLOCK])
        rowout = sb("rowout", [P, 4, TB, F])

        def rows_of(k):
            def at(lag):
                if k.peeled and k.c - lag == NB - 1:
                    return bass.ds(N - BLOCK, BLOCK)
                return bass.ds(k.n(lag) * BLOCK, BLOCK)
            return at

        def node_phase(final):
            m = NMLP - 1 if final else 0
            name = "f_" if final else "n_"
            LAG = 4
            AHEAD = 3
            with ExitStack() as own:
                def psem(nm):
                    return own.enter_context(nc.semaphore(name + nm))
                x_in = [psem(f"x_in{i}") for i in range(4)]
                y_in = [psem(f"y_in{i}") for i in range(4)]
                stored = [psem(f"stored{i}") for i in range(4)]
                st_done, mv_done, ve_done, rstd_done, norm_done = (psem(s) for s in ("stats_done", "meanvar_done", "vareps_done", "rstd_done", "norm_done"))
                xT_done, hT_done, s1_done, a_done, s2_done = (psem(s) for s in ("xT_done", "hT_done", "s1_done", "a_done", "s2_done"))
                b_done, h2_done, s3_done, o_done, row_done = (psem(s) for s in ("b_done", "h2_done", "s3_done", "o_done", "row_done"))

                passed = psem("waits_passed")

                def steps(eng, body):
                    run_steps(eng, body, 4, NB, LAG + 3, LAG, AHEAD)

                with nc.Block() as block:
                    @block.sync
                    def _(sp):
                        def load(k, lag):
                            if k.live(lag):
                                at, s = rows_of(k)(lag), k.slot(lag)
                                if final:
                                    if k.has(lag + 4):
                                        sp.wait_ge(xT_done, k.n(lag + 3))
                                        alone(sp, passed)
                                        sp.wait_ge(row_done, k.n(lag + 3))
                                        alone(sp, passed)
                                    sp.dma_start(yin[:, s, :, :], xb_view(at, ysum)).then_inc(y_in[s], 16)
                                elif k.has(lag + 4):
                                    sp.wait_ge(norm_done, k.n(lag + 3))
                                    alone(sp, passed)
                                sp.dma_start(xin[:, s, :, :], xb_view(at, x)).then_inc(x_in[s], 16)

                        def body(k):
                            if k.peeled and k.c == 0:
                                load(k, 0)
                                load(k, -1)
                            load(k, -2)
                            if k.live(LAG):
                                s = k.slot(LAG)
                                sp.wait_ge(row_done, k.n(LAG - 1))
                                alone(sp, passed)
                                if k.peeled and k.c - LAG == NB - 1:
                                    for lag in range(1, 4):
                                        sp.wait_ge(stored[k.slot(LAG + lag)], k.uses(LAG + lag) * 16)
                                sp.dma_start(xb_view(rows_of(k)(LAG), out if final else ysum), rowout[:, s, :, :]).then_inc(stored[s], 16)
                        steps(sp, body)
                        for b in range(max(NB - 4, 0), NB):
                            sp.wait_ge(stored[b % 4], 16 * (b // 4 + 1))

                    if not final:
                        @block.gpsimd
                        def _(pool):
                            def body(k):
                                if k.live(-2):
                                    s = k.slot(-2)
                                    pool.wait_ge(mv_done, k.n(-3))
                                    alone(pool, passed)
                                    nc.gpsimd.tensor_scalar(ve[:, s, :], mv[:, s, :, 1], EPS, None, ALU.add).then_inc(ve_done, 1)
                                    pool.wait_ge(ve_done, k.n(-3))
                                    nc.gpsimd.tensor_tensor(rstd[:, s, :], ve[:, s, :], neghalf[:, :], ALU.pow).then_inc(rstd_done, 1)
                            first = Step(0, -1, 4, NB)
                            body(Step(0, -2, 4, NB))
                            body(first)
                            steps(pool, body)

                    @block.vector
                    def _(dve):
                        def stats_of(k, lag):
                            if k.live(lag):
                                s = k.slot(lag)
                                dve.wait_ge(x_in[s], k.uses(lag) * 16)
                                for j in range(TB):
                                    last = nc.vector.bn_stats(stats[:, s, j, :], xin[:, s, j, :])
                                last.then_inc(st_done, 1)

                        def aggregate(k, lag):
                            if k.live(lag):
                                s = k.slot(lag)
                                dve.wait_ge(st_done, k.n(lag - 1))
                                alone(dve, passed)
                                for j in range(TB):
                                    last = nc.vector.bn_aggr(mv[:, s, j, :], stats[:, s, j, :])
                                last.then_inc(mv_done, 1)

                        def normalise(k, lag):
                            if k.live(lag):
                                s = k.slot(lag)
                                dve.wait_ge(rstd_done, k.n(lag - 1))
                                for j in range(TB):
                                    last = nc.vector.tensor_scalar(xn[:, s, j, :], xin[:, s, j, :], mv[:, s, j, 0:1],
                                                                   rstd[:, s, j:j + 1], ALU.subtract, ALU.mult)
                                last.then_inc(norm_done, 1)

                        def body(k):
                            s = k.slot()
                            if not final and k.peeled and k.c == 0:
                                for lag in (0, -1):
                                    stats_of(k, lag)
                                    aggregate(k, lag)
                                normalise(k, 0)
                            if k.live():
                                dve.wait_ge(xT_done, k.n(-1))
                                if k.has(4):
                                    dve.wait_ge(s1_done, k.n(3))
                                if final:
                                    nc.vector.tensor_copy(hT[:, s, :], psum[0][:, :]).then_inc(hT_done, 1)
                                else:
                                    nc.vector.tensor_scalar_max(hT[:, s, :], psum[0][:, :], 0.0).then_inc(hT_done, 1)
                            if not final:
                                stats_of(k, -2)
                            if k.live(2):
                                q = k.slot(2)
                                dve.wait_ge(b_done, k.n(1))
                                dve.wait_ge(hT_done, k.n(1))
                                if k.has(6):
                                    dve.wait_ge(s3_done, k.n(5))
                                nc.vector.scalar_tensor_tensor(out=h2[:, q, :], in0=psum[2][:, :], scalar=b2_sb[:, m:m + 1],
                                                               in1=hT[:, q, :], op0=ALU.add, op1=ALU.add).then_inc(h2_done, 1)
                            if not final:
                                aggregate(k, -2)
                                normalise(k, -1)
                            elif k.live(3):
                                q = k.slot(3)
                                dve.wait_ge(o_done, k.n(2))
                                dve.wait_ge(x_in[q], k.uses(3) * 16)
                                if k.has(7):
                                    dve.wait_ge(stored[q], k.uses(7) * 16)
                                nc.vector.tensor_tensor(rowout[:, q, :, :].rearrange("p t f -> p (t f)"), psum[3][:, :],
                                                        xin[:, q, :, :].rearrange("p t f -> p (t f)"), ALU.add).then_inc(row_done, 1)
                        steps(dve, body)

                    @block.scalar
                    def _(act):
                        def body(k):
                            if k.live():
                                s = k.slot()
                                act.wait_ge(hT_done, k.n(-1))
                                if k.has(4):
                                    act.wait_ge(a_done, k.n(3))
                                nc.scalar.activation(s1[:, s, :], hT[:, s, :], ACT.Silu).then_inc(s1_done, 1)
                            if k.live(1):
                                s = k.slot(1)
                                act.wait_ge(a_done, k.n(0))
                                if k.has(5):
                                    act.wait_ge(b_done, k.n(4))
                                nc.scalar.activation(s2[:, s, :], psum[1][:, :], ACT.Silu, bias=b1_sb[:, m:m + 1]).then_inc(s2_done, 1)
                            if k.live(2):
                                s = k.slot(2)
                                act.wait_ge(h2_done, k.n(1))
                                if k.has(6):
                                    act.wait_ge(o_done, k.n(5))
                                nc.scalar.activation(s3[:, s, :], h2[:, s, :], ACT.Silu).then_inc(s3_done, 1)
                            if not final and k.live(3):
                                s = k.slot(3)
                                act.wait_ge(o_done, k.n(2))
                                if k.has(7):
                                    act.wait_ge(stored[s], k.uses(7) * 16)
                                nc.scalar.copy(rowout[:, s, :, :].rearrange("p t f -> p (t f)"), psum[3][:, :]).then_inc(row_done, 1)
                        steps(act, body)

                    @block.tensor
                    def _(pe):
                        def body(k):
                            if k.live():
                                s = k.slot()
                                if final:
                                    pe.wait_ge(y_in[s], k.uses() * 16)
                                else:
                                    pe.wait_ge(norm_done, k.n(-1))
                                if k.has(1):
                                    pe.wait_ge(hT_done, k.n(0))
                                for j in range(TB):
                                    last = nc.tensor.transpose(psum[0][:, j * P:(j + 1) * P], (yin if final else xn)[:, s, j, :], ident[:, :])
                                last.then_inc(xT_done, 1)
                            if k.live(1):
                                s = k.slot(1)
                                pe.wait_ge(s1_done, k.n(0))
                                if k.has(2):
                                    pe.wait_ge(s2_done, k.n(1))
                                nc.tensor.matmul(psum[1][:, :], w1_sb[:, m, :], s1[:, s, :], start=True, stop=True).then_inc(a_done, 1)
                            if k.live(2):
                                s = k.slot(2)
                                pe.wait_ge(s2_done, k.n(1))
                                if k.has(3):
                                    pe.wait_ge(h2_done, k.n(2))
                                nc.tensor.matmul(psum[2][:, :], w2_sb[:, m, :], s2[:, s, :], start=True, stop=True).then_inc(b_done, 1)
                            if k.live(3):
                                s = k.slot(3)
                                pe.wait_ge(s3_done, k.n(2))
                                if k.has(4):
                                    pe.wait_ge(row_done, k.n(3))
                                for j in range(TB):
                                    last = nc.tensor.matmul(psum[3][:, j * P:(j + 1) * P], s3[:, s, j * P:(j + 1) * P], wo_sb[:, m, :],
                                                            start=True, stop=True)
                                last.then_inc(o_done, 1)
                        steps(pe, body)

        node_phase(False)
        edge_phase(nc, locals())
        node_phase(True)


def edge_phase(nc, env):
    fp32, i32 = mybir.dt.float32, mybir.dt.int32
    ALU = mybir.AluOpType
    ACT = mybir.ActivationFunctionType
    P, F, TB, V, R, G, KT, W, BLOCK, EPS = (env[n] for n in ("P", "F", "TB", "V", "R", "G", "KT", "W", "BLOCK", "EPS"))
    x, by_src, ysum, psum, sb = (env[n] for n in ("x", "by_src", "ysum", "psum", "sb"))
    ident, unit, trash, is_real, mask_p, mask_d, neghalf, zeros = (
        env[n] for n in ("ident", "unit", "trash", "is_real", "mask_p", "mask_d", "neghalf", "zeros"))
    w1_sb, w2_sb, wo_sb, b1_sb, b2_sb, wr_sb, wpp_sb, wpd_sb = (
        env[n] for n in ("w1_sb", "w2_sb", "wo_sb", "b1_sb", "b2_sb", "wr_sb", "wpp_sb", "wpd_sb"))
    xg, xn, stats, mv, ve, rstd, hT, s1, s2, h2, s3, urow = (
        env[n] for n in ("xin", "xn", "stats", "mv", "ve", "rstd", "hT", "s1", "s2", "h2", "s3", "rowout"))
    MLP = (2, 3, 1)
    V3 = 3 * V
    U = 3

    er = sb("er", [P, U, TB, W])
    nxt = sb("nxt", [P, U, TB], i32)
    srcf = sb("srcf", [P, U, TB])
    nxtf = sb("nxtf", [P, U, TB])
    ends = sb("ends", [P, U, TB])
    row_f = sb("row_f", [P, U, TB])
    row_i = sb("row_i", [P, U, TB], i32)
    eT = sb("eT", [KT, U, BLOCK])
    eTp = sb("eTp", [V3, U, BLOCK])
    eTd = sb("eTd", [V3, U, BLOCK])
    gate = sb("gate", [P, 3, BLOCK])
    mT = sb("mT", [P, U, 2, BLOCK])
    msg = sb("msg", [P, U, TB, F])
    AB = sb("AB", [P, 2, 4, F])
    same = sb("same", [P, 2, P])
    gram = sb("gram", [P, 2, 2, P])
    last_w = sb("last_w", [P, 2, V3])
    prod = sb("prod", [P, 2, 2, F])
    allsum = sb("allsum", [P, 2, 2, F])

    HT_AT_G, BANK_A, BANK_B, BANK_O, BANK_AB, BANK_SEG, BANK_C, BANK_TU = psum
    SRC_T, GRAM, S_CARRY = BANK_SEG[:, 0:P], BANK_SEG[:, P:3 * P], BANK_SEG[0:V, 3 * P:4 * P]
    BANK_T, BANK_U = BANK_TU[:, 0:2 * F], BANK_TU[:, 3 * F:4 * F]

    def tiles(dram_rows):
        return dram_rows.rearrange("(t r) w -> r t w", r=R)

    with ExitStack() as own:
        def sem(nm):
            return own.enter_context(nc.semaphore("e_" + nm))
        nxt_clear = sem("nxt_cleared")
        rows_in = [sem(f"edge_rows_in{i}") for i in range(U)]
        x_in = [sem(f"gathered{i}") for i in range(U)]
        added = [sem(f"added{i}") for i in range(TB)]
        unit_done, srcf_done, idx_a, idx_b, idx_c, row_done = (sem(s) for s in ("unit_done", "srcf_done", "idx_a", "idx_b", "idx_c", "rows_done"))
        st_done, mv_done, ve_done, rstd_done, norm_done = (sem(s) for s in ("stats_done", "meanvar_done", "vareps_done", "rstd_done", "norm_done"))
        xT_done, hT_done, s1_done, eT_ps, eT_done, eTm_done = (sem(s) for s in ("xT_done", "hT_done", "s1_done", "eT_in_psum", "eT_done", "eT_masked"))
        a_done, s2_done, b_done, h2_done, s3_done, g_ps, gate_done, o_done, msg_done = (
            sem(s) for s in ("a_done", "s2_done", "b_done", "h2_done", "s3_done", "gate_in_psum", "gate_done", "o_done", "msg_done"))
        seg_ps, ab_ps, ab_done, ab_carried, same_done, gram_done, lastw_done, c_done, ms_done = (
            sem(s) for s in ("seg_in_psum", "ab_in_psum", "ab_done", "ab_carried", "same_done", "gram_done", "last_weights_done", "carry_done", "sums_carried"))
        t_done, prod_done, sum1_done, sum_done, u_ps, u_done = (
            sem(s) for s in ("t_done", "prod_done", "sum1_done", "sum_done", "u_in_psum", "u_done"))

        passed = sem("waits_passed")

        def steps(eng, body):
            run_steps(eng, body, U, G, U + 1, 2, 1)

        def nm(k, lag, m, plus=0):
            return k.n(lag) * 3 + (m + plus)

        def nt(k, j, plus=0):
            return k.n(1) * TB + (j + plus)

        def first_tile(k, j, back):
            return k.peeled and (k.c - 1) * TB + j - back < 0

        def previous(k, j):
            return k.live(1 if j else 2)

        with nc.Block() as block:
            @block.sync
            def _(sp):
                sp.wait_ge(nxt_clear, 1)

                def load(k, lag):
                    if not k.live(lag):
                        return
                    s = k.slot(lag)
                    if k.has(lag + U):
                        sp.wait_ge(c_done, k.n(lag + U - 1) * TB)
                        alone(sp, passed)
                        sp.wait_ge(row_done, k.n(lag + U - 1))
                        alone(sp, passed)
                        sp.wait_ge(x_in[s], k.uses(lag + U) * 64)
                        alone(sp, passed)
                    start = k.n(lag) * (TB * R)
                    sp.dma_start(er[V:P, s, :, :], tiles(by_src[bass.ds(start + 1, TB * R), :])).then_inc(rows_in[s], 16)
                    sp.dma_start(er[0:V, s, :, :], tiles(by_src[bass.ds(start, TB * R), :])[0].partition_broadcast(V)).then_inc(rows_in[s], 16)
                    with nc.allow_non_contiguous_dma(reason="one word of each row"):
                        sp.dma_start(nxt[V:P, s, :], tiles(by_src[bass.ds(start + 2, TB * R), 0:1])[:, :, 0].bitcast(i32),
                                     allow_slow_non_contiguous=True).then_inc(rows_in[s], 16)

                def body(k):
                    if k.peeled and k.c == 0:
                        load(k, 0)
                    load(k, -1)
                steps(sp, body)

            @block.gpsimd
            def _(pool):
                nc.gpsimd.memset(nxt[:, :, :], 0).then_inc(nxt_clear, 1)

                def gather(k, lag):
                    if not k.live(lag):
                        return
                    s = k.slot(lag)
                    pool.wait_ge(rows_in[s], k.uses(lag) * 48)
                    alone(pool, passed)
                    nc.gpsimd.tensor_copy(er[0:V, s, :, 2:2 + V3], unit[:, :, :]).then_inc(unit_done, 1)
                    if k.has(lag + U):
                        pool.wait_ge(norm_done, k.n(lag + U - 1))
                        alone(pool, passed)
                    for j in range(TB):
                        nc.gpsimd.indirect_dma_start(
                            out=xg[:, s, j, :], out_offset=None, in_=x,
                            in_offset=bass.IndirectOffsetOnAxis(ap=er[:, s, j, 1:2].bitcast(i32), axis=0)).then_inc(x_in[s], 16)

                def scale(k, lag):
                    if k.live(lag):
                        s = k.slot(lag)
                        pool.wait_ge(mv_done, k.n(lag - 1))
                        alone(pool, passed)
                        nc.gpsimd.tensor_scalar(ve[:, s, :], mv[:, s, :, 1], EPS, None, ALU.add).then_inc(ve_done, 1)
                        pool.wait_ge(ve_done, k.n(lag - 1))
                        nc.gpsimd.tensor_tensor(rstd[:, s, :], ve[:, s, :], neghalf[:, :], ALU.pow).then_inc(rstd_done, 1)

                def add_row(k, j):
                    if previous(k, j):
                        b, s = (j - 1) % TB, k.slot(1 if j else 2)
                        pool.wait_ge(u_done, nt(k, j))
                        if not first_tile(k, j, 2):
                            pool.wait_ge(added[(j - 2) % TB], (k.n(0) if j > 1 else k.n(1)) * 16)
                        alone(pool, passed)
                        nc.gpsimd.indirect_dma_start(
                            out=ysum, out_offset=bass.IndirectOffsetOnAxis(ap=row_i[:, s, b:b + 1], axis=0),
                            in_=urow[:, b, 0, :], in_offset=None, compute_op=ALU.add).then_inc(added[b], 16)

                def body(k):
                    if k.peeled and k.c == 0:
                        gather(k, 0)
                        scale(k, 0)
                    gather(k, -1)
                    if k.live(0):
                        s = k.slot()
                        pool.wait_ge(eT_done, k.n(-1))
                        if k.has(U):
                            pool.wait_ge(seg_ps, k.n(U - 1) * TB)
                        alone(pool, passed)
                        nc.gpsimd.tensor_scalar(eTp[:, s, :], eT[0:V3, s, :], mask_p[0:V3, :], None, ALU.mult)
                        nc.gpsimd.tensor_scalar(eTd[:, s, :], eT[0:V3, s, :], mask_d[0:V3, :], None, ALU.mult).then_inc(eTm_done, 1)
                    for j in range(TB):
                        add_row(k, j)
                        if k.live(1):
                            s = k.slot(1)
                            pool.wait_ge(prod_done, nt(k, j, 1))
                            if not first_tile(k, j, 2):
                                pool.wait_ge(u_ps, nt(k, j, -1))
                            nc.gpsimd.tensor_tensor(allsum[:, j % 2, 0, :], prod[:, j % 2, 0, :], prod[:, j % 2, 1, :], ALU.add).then_inc(sum1_done, 1)
                            pool.wait_ge(sum1_done, nt(k, j, 1))
                            pool.wait_ge(ms_done, nt(k, j, 1))
                            nc.gpsimd.tensor_tensor(allsum[:, j % 2, 1, :], allsum[:, j % 2, 0, :], msg[:, s, j, :], ALU.add).then_inc(sum_done, 1)
                        if j == 1:
                            scale(k, -1)
                steps(pool, body)
                for j in range(TB):
                    pool.wait_ge(added[j], 16 * G)

            @block.vector
            def _(dve):
                def indices(k, lag):
                    if not k.live(lag):
                        return
                    s = k.slot(lag)
                    n = k.n(lag - 1)
                    dve.wait_ge(rows_in[s], k.uses(lag) * 48)
                    if k.has(lag + U):
                        dve.wait_ge(seg_ps, k.n(lag + U - 1) * TB)
                        dve.wait_ge(added[TB - 1], k.n(lag + U - 1) * 16)
                    nc.vector.tensor_copy(srcf[:, s, :], er[:, s, :, 0].bitcast(i32))
                    nc.vector.tensor_copy(nxtf[:, s, :], nxt[:, s, :]).then_inc(srcf_done, 1)
                    dve.wait_ge(srcf_done, n)
                    nc.vector.tensor_tensor(ends[:, s, :], srcf[:, s, :], nxtf[:, s, :], ALU.not_equal)
                    nc.vector.tensor_scalar(row_f[:, s, :], srcf[:, s, :], trash[:, 0:1], is_real[:, 0:1], ALU.subtract, ALU.mult).then_inc(idx_a, 1)
                    dve.wait_ge(idx_a, n)
                    nc.vector.tensor_tensor(nxtf[:, s, :], row_f[:, s, :], ends[:, s, :], ALU.mult).then_inc(idx_b, 1)
                    dve.wait_ge(idx_b, n)
                    nc.vector.tensor_scalar(row_i[:, s, :], nxtf[:, s, :], trash[:, 0:1], None, ALU.add).then_inc(row_done, 1)

                def stats_of(k, lag):
                    if k.live(lag):
                        s = k.slot(lag)
                        dve.wait_ge(x_in[s], k.uses(lag) * 64)
                        for j in range(TB):
                            last = nc.vector.bn_stats(stats[:, s, j, :], xg[:, s, j, :])
                        last.then_inc(st_done, 1)
                        dve.wait_ge(st_done, k.n(lag - 1))
                        alone(dve, passed)
                        for j in range(TB):
                            last = nc.vector.bn_aggr(mv[:, s, j, :], stats[:, s, j, :])
                        last.then_inc(mv_done, 1)

                def normalise(k, lag):
                    if k.live(lag):
                        s = k.slot(lag)
                        dve.wait_ge(rstd_done, k.n(lag - 1))
                        if k.has(lag + U):
                            dve.wait_ge(xT_done, k.n(lag + U - 1))
                        for j in range(TB):
                            last = nc.vector.tensor_scalar(xn[:, s, j, :], xg[:, s, j, :], mv[:, s, j, 0:1],
                                                           rstd[:, s, j:j + 1], ALU.subtract, ALU.mult)
                        last.then_inc(norm_done, 1)

                def residual(k, m):
                    if k.live():
                        dve.wait_ge(b_done, nm(k, 0, m, 1))
                        if k.has(1):
                            dve.wait_ge(s3_done, nm(k, 1, m, 1))
                        nc.vector.scalar_tensor_tensor(out=h2[:, m, :], in0=BANK_B[:, :], scalar=b2_sb[:, MLP[m]:MLP[m] + 1],
                                                       in1=hT[:, 0, :], op0=ALU.add, op1=ALU.add).then_inc(h2_done, 1)

                def message(k, m):
                    if k.live():
                        s = k.slot()
                        dve.wait_ge(o_done, nm(k, 0, m, 1))
                        dve.wait_ge(gate_done, nm(k, 0, m, 1))
                        if k.has(U):
                            dve.wait_ge(ab_ps if m < 2 else sum_done, k.n(U - 1) * TB)
                            if m == 2:
                                dve.wait_ge(c_done, k.n(U - 1) * TB)
                        dest = mT[:, s, m, :] if m < 2 else msg[:, s, :, :].rearrange("p t f -> p (t f)")
                        nc.vector.tensor_tensor(dest, BANK_O[:, :], gate[:, m, :], ALU.mult).then_inc(msg_done, 1)

                def seg_masks(k, j):
                    if k.live(1):
                        s, q = k.slot(1), j % 2
                        dve.wait_ge(seg_ps, nt(k, j, 1))
                        if not first_tile(k, j, 2):
                            dve.wait_ge(u_ps, nt(k, j, -1))
                            dve.wait_ge(t_done, nt(k, j, -1))
                            dve.wait_ge(c_done, nt(k, j, -1))
                        nc.vector.tensor_scalar(same[:, q, :], SRC_T, srcf[:, s, j:j + 1], None, ALU.is_equal).then_inc(same_done, 1)
                        dve.wait_ge(same_done, nt(k, j, 1))
                        nc.vector.tensor_tensor(gram[:, q, :, :], GRAM.rearrange("p (a b) -> p a b", a=2),
                                                same[:, q, :].unsqueeze(1).to_broadcast([P, 2, P]), ALU.mult).then_inc(gram_done, 1)
                        nc.vector.tensor_scalar(last_w[:, q, :], er[:, s, j, 2:2 + V3], same[:, q, P - 1:P], None, ALU.mult).then_inc(lastw_done, 1)

                def seg_carry(k, j):
                    if k.live(1):
                        s = k.slot(1)
                        dve.wait_ge(msg_done, k.n(0) * 3)
                        if first_tile(k, j, 1):
                            nc.vector.tensor_copy(msg[0:V, s, j, :], zeros[0:V, 0:F]).then_inc(ms_done, 1)
                        else:
                            dve.wait_ge(c_done, nt(k, j, 0))
                            nc.vector.tensor_copy(msg[0:V, s, j, :], S_CARRY).then_inc(ms_done, 1)

                def seg_prod(k, j):
                    if k.live(1):
                        q = j % 2
                        dve.wait_ge(t_done, nt(k, j, 1))
                        dve.wait_ge(ab_carried, nt(k, j, 1))
                        if not first_tile(k, j, 2):
                            dve.wait_ge(sum1_done, nt(k, j, -1))
                        nc.vector.tensor_tensor(prod[:, q, :, :], BANK_T.rearrange("p (a b) -> p a b", a=2),
                                                AB[:, q, :, :].rearrange("p (a b) f -> p a b f", b=2)[:, :, 0, :], ALU.mult).then_inc(prod_done, 1)

                def body(k):
                    if k.peeled and k.c == 0:
                        indices(k, 0)
                        stats_of(k, 0)
                        normalise(k, 0)
                    seg_carry(k, 0)
                    if k.live():
                        dve.wait_ge(xT_done, k.n(-1))
                        if k.has(1):
                            dve.wait_ge(s1_done, k.n(0))
                        nc.vector.tensor_scalar_max(hT[:, 0, :], HT_AT_G[:, :], 0.0).then_inc(hT_done, 1)
                    seg_masks(k, 0)
                    indices(k, -1)
                    seg_prod(k, 0)
                    seg_carry(k, 1)
                    seg_masks(k, 1)
                    residual(k, 0)
                    seg_carry(k, 2)
                    seg_prod(k, 1)
                    residual(k, 1)
                    message(k, 0)
                    seg_masks(k, 2)
                    stats_of(k, -1)
                    residual(k, 2)
                    seg_carry(k, 3)
                    seg_prod(k, 2)
                    message(k, 1)
                    normalise(k, -1)
                    seg_masks(k, 3)
                    message(k, 2)
                    seg_prod(k, 3)
                steps(dve, body)

            @block.scalar
            def _(act):
                def silu1(k):
                    if k.live():
                        act.wait_ge(hT_done, k.n(-1))
                        if k.has(1):
                            act.wait_ge(a_done, nm(k, 1, 2, 1))
                        nc.scalar.activation(s1[:, 0, :], hT[:, 0, :], ACT.Silu).then_inc(s1_done, 1)

                def silu2(k, m):
                    if k.live():
                        act.wait_ge(a_done, nm(k, 0, m, 1))
                        if k.has(1):
                            act.wait_ge(b_done, nm(k, 1, m, 1))
                        nc.scalar.activation(s2[:, m, :], BANK_A[:, :], ACT.Silu, bias=b1_sb[:, MLP[m]:MLP[m] + 1]).then_inc(s2_done, 1)

                def silu3(k, m):
                    if k.live():
                        act.wait_ge(h2_done, nm(k, 0, m, 1))
                        if k.has(1):
                            act.wait_ge(o_done, nm(k, 1, m, 1))
                        nc.scalar.activation(s3[:, m, :], h2[:, m, :], ACT.Silu).then_inc(s3_done, 1)

                def edges_T(k):
                    if k.live():
                        act.wait_ge(eT_ps, k.n(-1))
                        if k.has(U):
                            act.wait_ge(seg_ps, k.n(U - 1) * TB)
                        nc.scalar.copy(eT[:, k.slot(), :], HT_AT_G[0:KT, :]).then_inc(eT_done, 1)

                def gates(k, m):
                    if k.live():
                        act.wait_ge(g_ps, nm(k, 0, m, 1))
                        if k.has(1):
                            act.wait_ge(msg_done, nm(k, 1, m, 1))
                        nc.scalar.copy(gate[:, m, :], HT_AT_G[:, :]).then_inc(gate_done, 1)

                def halves(k, j):
                    if k.live(1):
                        q = j % 2
                        act.wait_ge(ab_ps, nt(k, j, 1))
                        if not first_tile(k, j, 2):
                            act.wait_ge(c_done, nt(k, j, -1))
                            act.wait_ge(t_done, nt(k, j, -1))
                            act.wait_ge(prod_done, nt(k, j, -1))
                        flat = AB[:, q, :, :].rearrange("p a f -> p (a f)")
                        nc.scalar.copy(flat, BANK_AB[:, :]).then_inc(ab_done, 1)
                        act.wait_ge(ab_done, nt(k, j, 1))
                        if first_tile(k, j, 1):
                            nc.scalar.copy(flat[0:V, :], zeros[0:V, :]).then_inc(ab_carried, 1)
                        else:
                            act.wait_ge(c_done, nt(k, j, 0))
                            nc.scalar.copy(flat[0:V, :], BANK_C[0:V, :]).then_inc(ab_carried, 1)

                def sums_out(k, j):
                    if previous(k, j):
                        b = (j - 1) % TB
                        act.wait_ge(u_ps, nt(k, j))
                        if not first_tile(k, j, TB + 1):
                            act.wait_ge(added[b], (k.n(1) if j else k.n(2)) * 16)
                        nc.scalar.copy(urow[:, b, 0, :], BANK_U).then_inc(u_done, 1)

                def body(k):
                    halves(k, 0)
                    silu1(k)
                    sums_out(k, 0)
                    edges_T(k)
                    silu2(k, 0)
                    gates(k, 0)
                    silu2(k, 1)
                    halves(k, 1)
                    silu3(k, 0)
                    sums_out(k, 1)
                    silu2(k, 2)
                    gates(k, 1)
                    silu3(k, 1)
                    halves(k, 2)
                    sums_out(k, 2)
                    silu3(k, 2)
                    gates(k, 2)
                    halves(k, 3)
                    sums_out(k, 3)
                steps(act, body)

            @block.tensor
            def _(pe):
                def rows_T(k):
                    if k.live():
                        pe.wait_ge(norm_done, k.n(-1))
                        if k.has(1):
                            pe.wait_ge(gate_done, nm(k, 1, 2, 1))
                        for j in range(TB):
                            last = nc.tensor.transpose(HT_AT_G[:, j * P:(j + 1) * P], xn[:, k.slot(), j, :], ident[:, :])
                        last.then_inc(xT_done, 1)

                def edges_T(k):
                    if k.live():
                        pe.wait_ge(unit_done, k.n(-1))
                        pe.wait_ge(rows_in[k.slot()], k.uses() * 48)
                        pe.wait_ge(hT_done, k.n(-1))
                        alone(pe, passed)
                        for j in range(TB):
                            last = nc.tensor.transpose(HT_AT_G[0:KT, j * P:(j + 1) * P], er[:, k.slot(), j, 2:W], ident[:, :])
                        last.then_inc(eT_ps, 1)

                def up(k, m):
                    if k.live():
                        pe.wait_ge(s1_done, k.n(-1))
                        if m or k.has(1):
                            pe.wait_ge(s2_done, nm(k, 0, m, 0))
                        nc.tensor.matmul(BANK_A[:, :], w1_sb[:, MLP[m], :], s1[:, 0, :], start=True, stop=True).then_inc(a_done, 1)

                def down(k, m):
                    if k.live():
                        pe.wait_ge(s2_done, nm(k, 0, m, 1))
                        if m or k.has(1):
                            pe.wait_ge(h2_done, nm(k, 0, m, 0))
                        nc.tensor.matmul(BANK_B[:, :], w2_sb[:, MLP[m], :], s2[:, m, :], start=True, stop=True).then_inc(b_done, 1)

                def gates(k, m):
                    if k.live():
                        pe.wait_ge(eT_done, k.n(-1))
                        if m:
                            pe.wait_ge(gate_done, nm(k, 0, m, 0))
                        if m < 2:
                            last = nc.tensor.matmul(HT_AT_G[:, :], wr_sb[:, m, :], eT[:, k.slot(), :], start=True, stop=True)
                        else:
                            for j in range(TB):
                                last = nc.tensor.matmul(HT_AT_G[:, j * P:(j + 1) * P], eT[:, k.slot(), j * P:(j + 1) * P], wr_sb[:, m, :], start=True, stop=True)
                        last.then_inc(g_ps, 1)

                def outp(k, m):
                    if k.live():
                        pe.wait_ge(s3_done, nm(k, 0, m, 1))
                        if m or k.has(1):
                            pe.wait_ge(msg_done, nm(k, 0, m, 0))
                        if m < 2:
                            last = nc.tensor.matmul(BANK_O[:, :], wo_sb[:, MLP[m], :], s3[:, m, :], start=True, stop=True)
                        else:
                            for j in range(TB):
                                last = nc.tensor.matmul(BANK_O[:, j * P:(j + 1) * P], s3[:, m, j * P:(j + 1) * P], wo_sb[:, MLP[m], :], start=True, stop=True)
                        last.then_inc(o_done, 1)

                def seg(k, j):
                    if k.live(1):
                        s, cols = k.slot(1), slice(j * P, (j + 1) * P)
                        pe.wait_ge(eTm_done, k.n(0))
                        pe.wait_ge(row_done, k.n(0))
                        if not first_tile(k, j, 1):
                            pe.wait_ge(gram_done, nt(k, j))
                        pe.wait_ge(ms_done, nt(k, j, 1))
                        nc.tensor.transpose(SRC_T, srcf[:, s, j:j + 1].to_broadcast([P, P]), ident[:, :])
                        nc.tensor.matmul(GRAM[:, 0:P], eTp[:, s, cols], eT[0:V3, s, cols], start=True, stop=True)
                        nc.tensor.matmul(GRAM[:, P:2 * P], eTd[:, s, cols], eT[0:V3, s, cols], start=True, stop=True).then_inc(seg_ps, 1)

                def halves(k, j):
                    if k.live(1):
                        s, cols = k.slot(1), slice(j * P, (j + 1) * P)
                        pe.wait_ge(msg_done, nm(k, 1, 1, 1))
                        if not first_tile(k, j, 1):
                            pe.wait_ge(ab_done, nt(k, j, 0))
                        nc.tensor.matmul(BANK_AB[:, 0:2 * F], mT[:, s, 0, cols], wpp_sb[:, :], start=True, stop=True)
                        nc.tensor.matmul(BANK_AB[:, 2 * F:4 * F], mT[:, s, 1, cols], wpd_sb[:, :], start=True, stop=True).then_inc(ab_ps, 1)

                def carry(k, j):
                    if k.live(1):
                        s, q = k.slot(1), j % 2
                        pe.wait_ge(lastw_done, nt(k, j, 1))
                        pe.wait_ge(ab_carried, nt(k, j, 1))
                        pe.wait_ge(ms_done, nt(k, j, 1))
                        flat = AB[:, q, :, :].rearrange("p a f -> p (a f)")
                        nc.tensor.matmul(BANK_C[0:V, 0:2 * F], last_w[:, q, V:2 * V], flat[:, 0:2 * F], start=True, stop=True)
                        nc.tensor.matmul(BANK_C[0:V, 2 * F:4 * F], last_w[:, q, 2 * V:V3], flat[:, 2 * F:4 * F], start=True, stop=True)
                        nc.tensor.matmul(S_CARRY, last_w[:, q, 0:V], msg[:, s, j, :], start=True, stop=True).then_inc(c_done, 1)

                def inner(k, j):
                    if k.live(1):
                        q = j % 2
                        pe.wait_ge(gram_done, nt(k, j, 1))
                        if not first_tile(k, j, 1):
                            pe.wait_ge(u_done, nt(k, j))
                        nc.tensor.matmul(BANK_T[:, 0:F], gram[:, q, 0, :], AB[:, q, 1, :], start=True, stop=True)
                        nc.tensor.matmul(BANK_T[:, F:2 * F], gram[:, q, 1, :], AB[:, q, 3, :], start=True, stop=True).then_inc(t_done, 1)

                def sums(k, j):
                    if previous(k, j):
                        q = (j - 1) % 2
                        pe.wait_ge(sum_done, nt(k, j))
                        nc.tensor.matmul(BANK_U, same[:, q, :], allsum[:, q, 1, :], start=True, stop=True).then_inc(u_ps, 1)

                def body(k):
                    rows_T(k)
                    seg(k, 0)
                    halves(k, 0)
                    sums(k, 0)
                    edges_T(k)
                    up(k, 0)
                    carry(k, 0)
                    inner(k, 0)
                    gates(k, 0)
                    up(k, 1)
                    seg(k, 1)
                    halves(k, 1)
                    down(k, 0)
                    sums(k, 1)
                    up(k, 2)
                    carry(k, 1)
                    inner(k, 1)
                    gates(k, 1)
                    down(k, 1)
                    outp(k, 0)
                    seg(k, 2)
                    halves(k, 2)
                    sums(k, 2)
                    down(k, 2)
                    carry(k, 2)
                    inner(k, 2)
                    outp(k, 1)
                    gates(k, 2)
                    seg(k, 3)
                    halves(k, 3)
                    sums(k, 3)
                    outp(k, 2)
                    carry(k, 3)
                    inner(k, 3)
                steps(pe, body)


_PRE = "L0_gnn_"
_INS = ["x", "src", "dst", "edge_attr_3", "edge_attr_32", "edge_attr_5"] + [
    _PRE + n for n in ("w_rs", "w_rp", "w_rd", "w_pp", "w_pd", "res_w1", "res_b1", "res_w2", "res_b2", "res_wout")]


def kernel(**inputs):
    import numpy as _np
    import concourse.bacc as _bacc
    from concourse import mybir as _mybir
    from concourse.bass_utils import run_bass_kernel_spmd as _run

    nc = _bacc.Bacc("TRN2", target_bir_lowering=False, num_devices=1)
    arrays, args = {}, []
    for name in _INS:
        a = _np.ascontiguousarray(inputs[name])
        arrays[f"in_{name}_dram"] = a
        args.append(nc.dram_tensor(f"in_{name}_dram", a.shape, _mybir.dt.from_np(a.dtype), kind="ExternalInput").ap())
    out = nc.dram_tensor("out_0_dram", inputs["x"].shape, _mybir.dt.float32, kind="ExternalOutput").ap()
    gnn_kernel(nc, *args, out)
    r = _run(nc, [arrays], core_ids=[0])
    return r.results[0]["out_0_dram"]
```

```python
import concourse.bass as bass
from concourse import mybir
from contextlib import ExitStack


class Step:

    def __init__(self, i, c, unroll, total):
        if isinstance(i, int):
            i, c = 0, i * unroll + c
        self.i, self.c, self.unroll, self.total = i, c, unroll, total
        self.peeled = isinstance(i, int)

    def live(self, lag=0):
        return not self.peeled or 0 <= self.c - lag < self.total

    def has(self, lag):
        return not self.peeled or self.c - lag >= 0

    def n(self, lag=0):
        return self.i * self.unroll + (self.c - lag)

    def slot(self, lag=0):
        return (self.c - lag) % self.unroll

    def uses(self, lag=0):
        return self.i + (self.c - lag) // self.unroll + 1


def alone(eng, passed):
    eng.sem_inc(passed, 1)


def run_steps(eng, body, unroll, total, first, last_lag, ahead, parts=(), beside=None):
    begin = -(-first // unroll)
    end = (total - ahead) // unroll
    for c in range(begin * unroll):
        body(Step(0, c, unroll, total))
    for n, count in enumerate([*parts, end - begin - sum(parts)]):
        if beside:
            beside.before(n)
        with eng.Fori(begin, begin + count) as i:
            for c in range(unroll):
                body(Step(i, c, unroll, total))
                if beside:
                    beside.during(n, i - begin, c)
        begin += count
    for c in range(end * unroll, total + last_lag):
        body(Step(0, c, unroll, total))


class Beside:

    def __init__(self, before, during):
        self.before, self.during = before, during


def gnn_kernel(nc, x, src, dst, attr3, attr32, attr5, w_rs, w_rp, w_rd, w_pp, w_pd,
               w1, b1, w2, b2, wout, out):
    fp32, i32, bf16 = mybir.dt.float32, mybir.dt.int32, mybir.dt.bfloat16
    ALU = mybir.AluOpType
    ACT = mybir.ActivationFunctionType
    AX = mybir.AxisListType

    P = 128
    N, F = x.shape
    E = src.shape[0]
    NRBF, NP3, ND5, NMLP = attr32.shape[1], attr3.shape[1], attr5.shape[1], w1.shape[0]
    EPS = 1e-5

    TB = 4
    BLOCK = TB * P
    NB = -(-N // BLOCK)

    PICKS = 5
    SORT_ITERATIONS = -(-E // (P * 4 * PICKS))
    T = SORT_ITERATIONS * 4 * PICKS
    SORT_PARTS = [1, SORT_ITERATIONS - 1, 1, SORT_ITERATIONS]
    FULL_P = E // T
    REST = E - FULL_P * T

    V = 5
    R = P - V
    G = -(-(-(-E // R)) // TB)
    ROWS = G * TB * R
    C_ONE, C_P, C_D, C_RBF = 0, V, 2 * V, 3 * V
    KT = 3 * V + NRBF
    W = 2 + KT
    SRC_ROWS = max(ROWS + 2, P * T + 1)
    PAD = N
    LOW = 256

    xb_view = lambda row, dram: dram[row, :].rearrange("(p t) f -> p t f", t=TB)

    ctx = ExitStack()
    with ctx:
        def sb(name, shape, dt=fp32):
            return ctx.enter_context(nc.sbuf_tensor(name, shape, dt))

        def sem(name):
            return ctx.enter_context(nc.semaphore(name))

        by_low = nc.dram_tensor("edges_by_low", [P * T, W], fp32, kind="Internal").ap()
        by_src = nc.dram_tensor("edges_by_src", [SRC_ROWS, W], fp32, kind="Internal").ap()
        ysum = nc.dram_tensor("node_sums", [N + P, F], fp32, kind="Internal").ap()

        ident = sb("ident", [P, P])
        ident_h = sb("ident_h", [P, P], bf16)
        before_h = sb("before_h", [P, P], bf16)
        ones_h = sb("ones_h", [P, P], bf16)
        digits_h = sb("digits_h", [P, LOW], bf16)
        column = sb("column", [P, LOW])
        part = sb("part", [P, 1])
        trash = sb("trash", [P, 1])
        is_real = sb("is_real", [P, 1])
        mask_p = sb("mask_p", [P, 1])
        mask_d = sb("mask_d", [P, 1])
        ge = sb("ge", [P, 4])
        neghalf = sb("neghalf", [P, TB])
        unit = sb("unit", [V, TB, 3 * V])
        w1_sb = sb("w1_sb", [P, NMLP, F])
        w2_sb = sb("w2_sb", [P, NMLP, F])
        wo_sb = sb("wo_sb", [P, NMLP, F])
        b1_sb = sb("b1_sb", [P, NMLP])
        b2_sb = sb("b2_sb", [P, NMLP])
        wr_sb = sb("wr_sb", [KT, 3, F])
        wpp_sb = sb("wpp_sb", [P, 2 * F])
        wpd_sb = sb("wpd_sb", [P, 2 * F])
        zeros = sb("zeros", [P, 4 * F])

        psum = [ctx.enter_context(nc.psum_tensor(f"bank{i}", [P, 512], fp32)) for i in range(8)]

        xin = sb("xin", [P, 4, TB, F])
        yin = sb("yin", [P, 4, TB, F])
        xn = sb("xn", [P, 4, TB, F])
        stats = sb("stats", [P, 4, TB, 6])
        mv = sb("mv", [P, 4, TB, 2])
        ve = sb("ve", [P, 4, TB])
        rstd = sb("rstd", [P, 4, TB])
        hT = sb("hT", [P, 4, BLOCK])
        s1 = sb("s1", [P, 4, BLOCK])
        s2 = sb("s2", [P, 4, BLOCK])
        h2 = sb("h2", [P, 4, BLOCK])
        s3 = sb("s3", [P, 4, BLOCK])
        rowout = sb("rowout", [P, 4, TB, F])

        own = ctx.enter_context(ExitStack())

        def psb(name, shape, dt=fp32):
            return own.enter_context(nc.sbuf_tensor(name, shape, dt))

        def psem(name):
            return own.enter_context(nc.semaphore(name))

        pay = psb("pay", [P, T, W])
        st_src = psb("st_src", [P, T], i32)
        st_dst = psb("st_dst", [P, T], i32)
        st3 = psb("st3", [P, T, NP3])
        st5 = psb("st5", [P, T, ND5])
        st32 = psb("st32", [P, T, NRBF])
        digit_i = psb("digit_i", [P, T], i32)
        digit_f = psb("digit_f", [P, T])
        onehot = psb("onehot", [P, T + 1, LOW], bf16)
        total = psb("total", [P, LOW])
        upto = psb("upto", [P, LOW])
        base = psb("base", [P, LOW])
        picked = psb("picked", [P, 2, LOW])
        rank_f = psb("rank_f", [P, 2])
        rank_i = psb("rank_i", [P, 4 * PICKS], i32)
        leaving = psb("leaving", [P, 4 * PICKS, W])
        padrow = psb("padrow", [P, 3, W])
        leadrow = psb("leadrow", [1, W])

        s_w = psem("weights_in")
        s_cst = psem("constants_made")
        s_dc = psem("dve_constants")
        s_staged = psem("stages_cleared")
        s_edges = psem("edges_in")
        s_pay = psem("payload_made")
        s_init = psem("tables_initialised")
        s_dig = psem("digits_made")
        s_alone = psem("pool_waits_passed")
        s_oh = psem("onehots_made")
        s_cnt = psem("counts_done")
        s_dve = psem("dve_chain")
        s_base = psem("bases_made")
        s_seed = psem("bases_added")
        s_pick = psem("ranks_picked")
        s_rank = psem("rank_indices_made")
        s_scat = [psem(f"scattered{i}") for i in range(4 * PICKS)]
        s_back = psem("sorted_by_low_in")
        s_leave = psem("tiles_leaving")

        groups = []
        at = P * T + 1
        left = max(SRC_ROWS - at, 0)
        while left:
            each = 3 if left >= 3 else 1
            parts = min(P, left // each)
            groups.append((at, parts, each))
            at += parts * each
            left -= parts * each

        def load_parts(dram, tile, eng, s, per):
            n = 0
            cut = FULL_P // 16 * 16
            flat = dram.rearrange("e c -> (e c)") if len(dram.shape) == 2 else dram
            for lo, hi, size in ((0, cut, T), (cut, FULL_P, T), (FULL_P, FULL_P + 1, REST)):
                if hi > lo and size:
                    first = lo * T * per
                    eng.dma_start(tile[lo:hi, 0:size * per],
                                  flat[first:first + (hi - lo) * size * per].rearrange("(p c) -> p c", p=hi - lo)).then_inc(s, 16)
                    n += 1
            return n

        n_edge_loads = [0]
        with nc.Block() as block:
            @block.sync
            def _(sp):
                sp.dma_start(w1_sb[:, :, :], w1.rearrange("m k n -> k m n")).then_inc(s_w, 16)
                sp.dma_start(w2_sb[:, :, :], w2.rearrange("m k n -> k m n")).then_inc(s_w, 16)
                sp.dma_start(wo_sb[:, :, :], wout.rearrange("m k n -> k m n")).then_inc(s_w, 16)
                for m in range(NMLP):
                    sp.dma_start(b1_sb[:, m:m + 1], b1[m:m + 1, :].rearrange("o k -> k o")).then_inc(s_w, 16)
                    sp.dma_start(b2_sb[:, m:m + 1], b2[m:m + 1, :].rearrange("o k -> k o")).then_inc(s_w, 16)
                sp.dma_start(wpp_sb[:, :], w_pp).then_inc(s_w, 16)
                sp.dma_start(wpd_sb[:, :], w_pd).then_inc(s_w, 16)
                sp.wait_ge(s_staged, 1)
                for dram, tile, per in ((src, st_src, 1), (dst, st_dst, 1), (attr3, st3, NP3), (attr5, st5, ND5), (attr32, st32, NRBF)):
                    flat = tile[:, :] if per == 1 else tile[:, :, :].rearrange("p t c -> p (t c)")
                    n_edge_loads[0] += load_parts(dram, flat, sp, s_edges, per)
                sp.dma_start(wr_sb[C_RBF:KT, 0, :], w_rp).then_inc(s_w, 16)
                sp.dma_start(wr_sb[C_RBF:KT, 1, :], w_rd).then_inc(s_w, 16)
                sp.dma_start(wr_sb[C_RBF:KT, 2, :], w_rs).then_inc(s_w, 16)
                sp.dma_start(by_src[0:1, :], leadrow[:, :]).then_inc(s_init, 16)
                for row, parts, each in groups:
                    sp.dma_start(by_src[row:row + parts * each, :].rearrange("(p t) w -> p t w", t=each),
                                 padrow[0:parts, 0:each, :]).then_inc(s_init, 16)
                sp.dma_start(ysum[N:N + P, :], zeros[:, 0:F]).then_inc(s_init, 16)
                sp.wait_ge(s_w, 16 * (8 + 2 * NMLP))

            @block.gpsimd
            def _(pool):
                nc.gpsimd.memset(st_src[:, :], PAD)
                nc.gpsimd.memset(st_dst[:, :], 0)
                nc.gpsimd.memset(st3[:, :, :], 0.0)
                nc.gpsimd.memset(st5[:, :, :], 0.0)
                nc.gpsimd.memset(st32[:, :, :], 0.0)
                nc.gpsimd.memset(zeros[:, :], 0.0)
                nc.gpsimd.memset(padrow[:, :, :], 0.0)
                nc.gpsimd.memset(leadrow[:, :], 0.0)
                nc.gpsimd.memset(wr_sb[:, :, :], 0.0).then_inc(s_cst, 1)
                pool.wait_ge(s_cst, 1)
                nc.gpsimd.memset(padrow[:, :, 0:1].bitcast(i32), PAD)
                nc.gpsimd.memset(leadrow[:, 0:1].bitcast(i32), PAD + 1).then_inc(s_staged, 1)
                nc.gpsimd.iota(column[:, :], [[1, LOW]], base=0, channel_multiplier=0,
                               allow_small_or_imprecise_dtypes=True)
                nc.gpsimd.iota(part[:, :], [[0, 1]], base=0, channel_multiplier=1,
                               allow_small_or_imprecise_dtypes=True)
                nc.gpsimd.memset(neghalf[:, :], -0.5)
                nc.gpsimd.memset(ones_h[:, :], 1.0).then_inc(s_cst, 1)
                nc.gpsimd.memset(onehot[:, T:T + 1, :], 0.0)
                nc.gpsimd.memset(pay[:, :, :], 0.0).then_inc(s_cst, 1)

            @block.vector
            def _(dve):
                n_chain = [0]

                def link(ins):
                    n_chain[0] += 1
                    ins.then_inc(s_dve, 1)
                    dve.wait_ge(s_dve, n_chain[0])

                dve.wait_ge(s_cst, 2)
                nc.vector.tensor_copy(digits_h[:, :], column[:, :])
                nc.vector.tensor_scalar(ident_h[:, :], column[:, 0:P], part[:, 0:1], None, ALU.is_equal)
                nc.vector.tensor_scalar(before_h[:, :], column[:, 0:P], part[:, 0:1], None, ALU.is_gt)
                nc.vector.tensor_scalar(trash[:, :], part[:, :], float(N), None, ALU.add)
                nc.vector.tensor_scalar(is_real[:, :], part[:, :], float(V), None, ALU.is_ge)
                for n in range(3):
                    nc.vector.tensor_scalar(ge[:, n:n + 1], part[:, :], float((n + 1) * V), None, ALU.is_ge)
                link(nc.vector.tensor_scalar(ident[:, :], column[:, 0:P], part[:, 0:1], None, ALU.is_equal))
                nc.vector.tensor_tensor(mask_p[:, :], ge[:, 0:1], ge[:, 1:2], ALU.subtract)
                nc.vector.tensor_tensor(mask_d[:, :], ge[:, 1:2], ge[:, 2:3], ALU.subtract)
                link(nc.vector.memset(unit[:, :, :], 0.0))
                for t in range(TB):
                    nc.vector.memset(unit[:, t, 0:1], 1.0)
                    nc.vector.tensor_copy(unit[:, t, V:V + NP3], ident[0:V, 0:NP3])
                    last = nc.vector.tensor_copy(unit[:, t, 2 * V:2 * V + ND5], ident[0:V, 0:ND5])
                link(last)

        class Sort:

            def __init__(self):
                self.passes = {0: (0, 0), 1: (0, 1), 3: (1, 0)}
                self.n_chain = 0
                self.sync = Beside(self.sync_before, lambda *a: None)
                self.gpsimd = Beside(self.gpsimd_before, self.gpsimd_during)
                self.scalar = Beside(self.scalar_before, self.scalar_during)
                self.vector = Beside(self.vector_before, self.vector_during)
                self.tensor = Beside(self.tensor_before, self.tensor_during)

            def sync_before(self, part):
                if part == 3:
                    for s in s_scat:
                        nc.sync.wait_ge(s, 16 * SORT_ITERATIONS)
                    nc.sync.dma_start(pay[:, :, :], by_low.rearrange("(p t) w -> p t w", t=T)).then_inc(s_back, 16)

            def scalar_before(self, part):
                if part == 0:
                    act = nc.scalar
                    act.wait_ge(s_cst, 3)
                    act.wait_ge(s_edges, 16 * n_edge_loads[0])
                    nc.scalar.copy(pay[:, :, 2 + C_P:2 + C_P + NP3], st3[:, :, :])
                    nc.scalar.copy(pay[:, :, 2 + C_D:2 + C_D + ND5], st5[:, :, :])
                    nc.scalar.copy(pay[:, :, 2 + C_RBF:2 + C_RBF + NRBF], st32[:, :, :]).then_inc(s_pay, 1)
                    act.wait_ge(s_pay, 2)

                if part == 3:
                    nc.scalar.wait_ge(s_back, 16)

            def scalar_during(self, part, i, c):
                if part not in self.passes:
                    return
                (n, done), act = self.passes[part], nc.scalar
                i = i + done
                for j in range(PICKS):
                    slot = c * PICKS + j
                    if part:
                        act.wait_ge(s_scat[slot], (i + n * SORT_ITERATIONS) * 16)
                    nc.scalar.copy(leaving[:, slot, :], pay[:, i * (4 * PICKS) + slot, :]).then_inc(s_leave, 1)

            def gpsimd_before(self, part):
                if part == 3:
                    nc.gpsimd.wait_ge(s_init, 16 * (2 + len(groups)))

            def gpsimd_during(self, part, i, c):
                if part not in self.passes:
                    return
                n, done = self.passes[part]
                i = i + done
                for j in range(PICKS):
                    slot = c * PICKS + j
                    t = i * (4 * PICKS) + slot
                    nc.gpsimd.wait_ge(s_rank, t + (n * T + 1))
                    alone(nc.gpsimd, s_alone)
                    nc.gpsimd.wait_ge(s_leave, t + (n * T + 1))
                    alone(nc.gpsimd, s_alone)
                    nc.gpsimd.indirect_dma_start(
                        out=(by_low, by_src)[n],
                        out_offset=bass.IndirectOffsetOnAxis(ap=rank_i[:, slot:slot + 1], axis=0),
                        in_=leaving[:, slot, :], in_offset=None).then_inc(s_scat[slot], 16)

            def finish(self, pool):
                for s in s_scat:
                    pool.wait_ge(s, 2 * 16 * SORT_ITERATIONS)

            def link(self, ins):
                self.n_chain += 1
                ins.then_inc(s_dig, 1)
                nc.vector.wait_ge(s_dig, self.n_chain)

            def vector_before(self, part):
                if part not in (0, 3):
                    return
                n, dve = self.passes[part][0], nc.vector
                if n == 0:
                    dve.wait_ge(s_cst, 3)
                    dve.wait_ge(s_edges, 16 * n_edge_loads[0])
                    nc.vector.memset(pay[:, :, 2:3], 1.0)
                    nc.vector.tensor_copy(pay[:, :, 0:1].bitcast(i32), st_src[:, :].unsqueeze(2))
                    nc.vector.tensor_copy(pay[:, :, 1:2].bitcast(i32), st_dst[:, :].unsqueeze(2)).then_inc(s_pay, 1)
                    self.link(nc.vector.tensor_single_scalar(digit_i[:, :], st_src[:, :], LOW - 1, op=ALU.bitwise_and))
                else:
                    dve.wait_ge(s_back, 16)
                    self.link(nc.vector.tensor_single_scalar(digit_i[:, :], pay[:, :, 0].bitcast(i32), LOW.bit_length() - 1,
                                                        op=ALU.arith_shift_right))
                self.link(nc.vector.tensor_copy(digit_f[:, :], digit_i[:, :]))
                with dve.Fori(0, T) as t:
                    nc.vector.tensor_scalar(onehot[:, t, :], digits_h[:, :], digit_f[:, bass.ds(t, 1)], None,
                                            ALU.is_equal).then_inc(s_oh, 1)
                dve.wait_ge(s_cnt, n + 1)
                self.link(nc.vector.tensor_copy(total[:, :], psum[6][:, 0:LOW]))
                self.link(nc.vector.tensor_tensor_scan(upto[:, :], total[:, :], zeros[:, 0:LOW], 0.0, ALU.add, ALU.add))
                nc.vector.tensor_tensor(base[:, :], upto[:, :], total[:, :], ALU.subtract).then_inc(s_base, 1)

            def vector_during(self, part, i, c):
                if part not in self.passes:
                    return
                (n, done), dve = self.passes[part], nc.vector
                i = i + done
                for j in range(PICKS):
                    slot = c * PICKS + j
                    t, q = i * (4 * PICKS) + slot, slot % 2
                    dve.wait_ge(s_seed, t + (n * (T + 2) + 1))
                    nc.vector.scalar_tensor_tensor(
                        out=picked[:, q, :], in0=psum[4 + q][:, 0:LOW], scalar=1.0, in1=onehot[:, t, :],
                        op0=ALU.mult, op1=ALU.mult, accum_out=rank_f[:, q:q + 1]).then_inc(s_pick, 1)
                    dve.wait_ge(s_pick, t + (n * T + 1))
                    if part:
                        dve.wait_ge(s_scat[slot], (i + n * SORT_ITERATIONS) * 16)
                    nc.vector.tensor_scalar(rank_i[:, slot:slot + 1], rank_f[:, q:q + 1], float(n), None, ALU.add).then_inc(s_rank, 1)

            def tensor_before(self, part):
                if part not in (0, 3):
                    return
                n, pe = self.passes[part][0], nc.tensor
                start = dict(stop=True, skip_group_check=True)

                def count(t, first):
                    for bank, lhsT in ((4, before_h), (5, before_h), (6, ones_h)):
                        last = nc.tensor.matmul(psum[bank][:, 0:LOW], lhsT[:, :], onehot[:, t, :], start=first, **start)
                    return last
                pe.wait_ge(s_oh, n * T + 1)
                count(0, True)
                with pe.Fori(1, T - 1) as t:
                    pe.wait_ge(s_oh, t + (n * T + 1))
                    count(t, False)
                pe.wait_ge(s_oh, n * T + T)
                count(T - 1, False).then_inc(s_cnt, 1)
                pe.wait_ge(s_base, n + 1)
                nc.tensor.matmul(psum[4][:, 0:LOW], ident[:, :], base[:, :], start=False, **start).then_inc(s_seed, 1)
                nc.tensor.matmul(psum[5][:, 0:LOW], ident[:, :], base[:, :], start=False, **start)
                nc.tensor.matmul(psum[5][:, 0:LOW], ident_h[:, :], onehot[:, 0, :], start=False, **start).then_inc(s_seed, 1)

            def tensor_during(self, part, i, c):
                if part not in self.passes:
                    return
                (n, done), pe = self.passes[part], nc.tensor
                i = i + done
                for j in range(PICKS):
                    t, q = i * (4 * PICKS) + (c * PICKS + j), (c * PICKS + j) % 2
                    pe.wait_ge(s_pick, t + (n * T + 1))
                    nc.tensor.matmul(psum[4 + q][:, 0:LOW], ident_h[:, :], onehot[:, t, :], start=False, stop=True, skip_group_check=True)
                    nc.tensor.matmul(psum[4 + q][:, 0:LOW], ident_h[:, :], onehot[:, t + 1, :], start=False, stop=True,
                                     skip_group_check=True).then_inc(s_seed, 1)

        def rows_of(k):
            def at(lag):
                if k.peeled and k.c - lag == NB - 1:
                    return bass.ds(N - BLOCK, BLOCK)
                return bass.ds(k.n(lag) * BLOCK, BLOCK)
            return at

        def node_phase(final, sort=None):
            m = NMLP - 1 if final else 0
            name = "f_" if final else "n_"
            LAG = 4
            AHEAD = 4
            with ExitStack() as own:
                def psem(nm):
                    return own.enter_context(nc.semaphore(name + nm))
                x_in = [psem(f"x_in{i}") for i in range(4)]
                y_in = [psem(f"y_in{i}") for i in range(4)]
                stored = [psem(f"stored{i}") for i in range(4)]
                st_done, mv_done, ve_done, rstd_done, norm_done = (psem(s) for s in ("stats_done", "meanvar_done", "vareps_done", "rstd_done", "norm_done"))
                xT_done, hT_done, s1_done, a_done, s2_done = (psem(s) for s in ("xT_done", "hT_done", "s1_done", "a_done", "s2_done"))
                b_done, h2_done, s3_done, o_done, row_done = (psem(s) for s in ("b_done", "h2_done", "s3_done", "o_done", "row_done"))

                passed = psem("waits_passed")

                def steps(eng, body, between=None):
                    run_steps(eng, body, 4, NB, LAG + 4, LAG, AHEAD, SORT_PARTS if sort else [], between)

                with nc.Block() as block:
                    def store(eng, k):
                        if k.live(LAG):
                            s = k.slot(LAG)
                            eng.wait_ge(row_done, k.n(LAG - 1))
                            alone(eng, passed)
                            if k.peeled and k.c - LAG == NB - 1:
                                for lag in range(1, 4):
                                    eng.wait_ge(stored[k.slot(LAG + lag)], k.uses(LAG + lag) * 16)
                            eng.dma_start(xb_view(rows_of(k)(LAG), out if final else ysum), rowout[:, s, :, :]).then_inc(stored[s], 16)

                    @block.sync
                    def _(sp):
                        def load_x(k, lag):
                            if k.live(lag):
                                at, s = rows_of(k)(lag), k.slot(lag)
                                if k.has(lag + 4):
                                    sp.wait_ge(row_done if final else norm_done, k.n(lag + 3))
                                    alone(sp, passed)
                                sp.dma_start(xin[:, s, :, :], xb_view(at, x)).then_inc(x_in[s], 16)

                        def load_y(k, lag):
                            if k.live(lag):
                                at, s = rows_of(k)(lag), k.slot(lag)
                                if k.has(lag + 4):
                                    sp.wait_ge(xT_done, k.n(lag + 3))
                                    alone(sp, passed)
                                sp.dma_start(yin[:, s, :, :], xb_view(at, ysum)).then_inc(y_in[s], 16)

                        def body(k):
                            if final:
                                if k.peeled and k.c == 0:
                                    load_y(k, 0)
                                    load_y(k, -1)
                                load_y(k, -2)
                                load_x(k, 0)
                            else:
                                if k.peeled and k.c == 0:
                                    for n in range(3):
                                        load_x(k, -n)
                                load_x(k, -3)
                        steps(sp, body, sort.sync if sort else None)
                        for b in range(max(NB - 4, 0), NB):
                            sp.wait_ge(stored[b % 4], 16 * (b // 4 + 1))

                    if not final:
                        @block.gpsimd
                        def _(pool):
                            def body(k):
                                if k.live(-2):
                                    s = k.slot(-2)
                                    pool.wait_ge(mv_done, k.n(-3))
                                    alone(pool, passed)
                                    nc.gpsimd.tensor_scalar(ve[:, s, :], mv[:, s, :, 1], EPS, None, ALU.add).then_inc(ve_done, 1)
                                    pool.wait_ge(ve_done, k.n(-3))
                                    nc.gpsimd.tensor_tensor(rstd[:, s, :], ve[:, s, :], neghalf[:, :], ALU.pow).then_inc(rstd_done, 1)
                            first = Step(0, -1, 4, NB)
                            body(Step(0, -2, 4, NB))
                            body(first)
                            steps(pool, body, sort.gpsimd)
                            sort.finish(pool)

                    @block.vector
                    def _(dve):
                        def stats_of(k, lag):
                            if k.live(lag):
                                s = k.slot(lag)
                                dve.wait_ge(x_in[s], k.uses(lag) * 16)
                                for j in range(TB):
                                    last = nc.vector.bn_stats(stats[:, s, j, :], xin[:, s, j, :])
                                last.then_inc(st_done, 1)

                        def aggregate(k, lag):
                            if k.live(lag):
                                s = k.slot(lag)
                                dve.wait_ge(st_done, k.n(lag - 1))
                                alone(dve, passed)
                                for j in range(TB):
                                    last = nc.vector.bn_aggr(mv[:, s, j, :], stats[:, s, j, :])
                                last.then_inc(mv_done, 1)

                        def normalise(k, lag):
                            if k.live(lag):
                                s = k.slot(lag)
                                dve.wait_ge(rstd_done, k.n(lag - 1))
                                for j in range(TB):
                                    last = nc.vector.tensor_scalar(xn[:, s, j, :], xin[:, s, j, :], mv[:, s, j, 0:1],
                                                                   rstd[:, s, j:j + 1], ALU.subtract, ALU.mult)
                                last.then_inc(norm_done, 1)

                        def body(k):
                            s = k.slot()
                            if not final and k.peeled and k.c == 0:
                                for lag in (0, -1):
                                    stats_of(k, lag)
                                    aggregate(k, lag)
                                normalise(k, 0)
                            if final and k.live():
                                dve.wait_ge(xT_done, k.n(-1))
                                if k.has(4):
                                    dve.wait_ge(s1_done, k.n(3))
                                nc.vector.tensor_copy(hT[:, s, :], psum[0][:, :]).then_inc(hT_done, 1)
                            if not final:
                                stats_of(k, -2)
                            if k.live(2):
                                q = k.slot(2)
                                dve.wait_ge(b_done, k.n(1))
                                dve.wait_ge(hT_done, k.n(1))
                                if k.has(6):
                                    dve.wait_ge(s3_done, k.n(5))
                                nc.vector.scalar_tensor_tensor(out=h2[:, q, :], in0=psum[2][:, :], scalar=b2_sb[:, m:m + 1],
                                                               in1=hT[:, q, :], op0=ALU.add, op1=ALU.add).then_inc(h2_done, 1)
                            if not final:
                                aggregate(k, -2)
                                normalise(k, -1)
                            elif k.live(3):
                                q = k.slot(3)
                                dve.wait_ge(o_done, k.n(2))
                                dve.wait_ge(x_in[q], k.uses(3) * 16)
                                if k.has(7):
                                    dve.wait_ge(stored[q], k.uses(7) * 16)
                                nc.vector.tensor_tensor(rowout[:, q, :, :].rearrange("p t f -> p (t f)"), psum[3][:, :],
                                                        xin[:, q, :, :].rearrange("p t f -> p (t f)"), ALU.add).then_inc(row_done, 1)
                        steps(dve, body, sort.vector if sort else None)

                    @block.scalar
                    def _(act):
                        def relu(k):
                            if k.live():
                                s = k.slot()
                                act.wait_ge(xT_done, k.n(-1))
                                if k.has(4):
                                    act.wait_ge(h2_done, k.n(3))
                                nc.scalar.activation(hT[:, s, :], psum[0][:, :], ACT.Relu).then_inc(hT_done, 1)

                        def silu1(k):
                            if k.live():
                                s = k.slot()
                                act.wait_ge(hT_done, k.n(-1))
                                if k.has(4):
                                    act.wait_ge(a_done, k.n(3))
                                nc.scalar.activation(s1[:, s, :], hT[:, s, :], ACT.Silu).then_inc(s1_done, 1)

                        def body(k):
                            if not final:
                                relu(k)
                            else:
                                silu1(k)
                            if k.live(1):
                                s = k.slot(1)
                                act.wait_ge(a_done, k.n(0))
                                if k.has(5):
                                    act.wait_ge(b_done, k.n(4))
                                nc.scalar.activation(s2[:, s, :], psum[1][:, :], ACT.Silu, bias=b1_sb[:, m:m + 1]).then_inc(s2_done, 1)
                            if not final:
                                silu1(k)
                            if k.live(2):
                                s = k.slot(2)
                                act.wait_ge(h2_done, k.n(1))
                                if k.has(6):
                                    act.wait_ge(o_done, k.n(5))
                                nc.scalar.activation(s3[:, s, :], h2[:, s, :], ACT.Silu).then_inc(s3_done, 1)
                            if not final and k.live(3):
                                s = k.slot(3)
                                act.wait_ge(o_done, k.n(2))
                                if k.has(7):
                                    act.wait_ge(stored[s], k.uses(7) * 16)
                                nc.scalar.copy(rowout[:, s, :, :].rearrange("p t f -> p (t f)"), psum[3][:, :]).then_inc(row_done, 1)
                            store(act, k)
                        steps(act, body, sort.scalar if sort else None)

                    @block.tensor
                    def _(pe):
                        def body(k):
                            if k.live():
                                s = k.slot()
                                if final:
                                    pe.wait_ge(y_in[s], k.uses() * 16)
                                else:
                                    pe.wait_ge(norm_done, k.n(-1))
                                if k.has(1):
                                    pe.wait_ge(hT_done, k.n(0))
                                for j in range(TB):
                                    last = nc.tensor.transpose(psum[0][:, j * P:(j + 1) * P], (yin if final else xn)[:, s, j, :], ident[:, :])
                                last.then_inc(xT_done, 1)
                            if k.live(1):
                                s = k.slot(1)
                                pe.wait_ge(s1_done, k.n(0))
                                if k.has(2):
                                    pe.wait_ge(s2_done, k.n(1))
                                nc.tensor.matmul(psum[1][:, :], w1_sb[:, m, :], s1[:, s, :], start=True, stop=True).then_inc(a_done, 1)
                            if k.live(2):
                                s = k.slot(2)
                                pe.wait_ge(s2_done, k.n(1))
                                if k.has(3):
                                    pe.wait_ge(h2_done, k.n(2))
                                nc.tensor.matmul(psum[2][:, :], w2_sb[:, m, :], s2[:, s, :], start=True, stop=True).then_inc(b_done, 1)
                            if k.live(3):
                                s = k.slot(3)
                                pe.wait_ge(s3_done, k.n(2))
                                if k.has(4):
                                    pe.wait_ge(row_done, k.n(3))
                                for j in range(TB):
                                    last = nc.tensor.matmul(psum[3][:, j * P:(j + 1) * P], s3[:, s, j * P:(j + 1) * P], wo_sb[:, m, :],
                                                            start=True, stop=True)
                                last.then_inc(o_done, 1)
                        steps(pe, body, sort.tensor if sort else None)

        node_phase(False, Sort())
        own.close()
        edge_phase(nc, locals())
        node_phase(True)


def edge_phase(nc, env):
    fp32, i32 = mybir.dt.float32, mybir.dt.int32
    ALU = mybir.AluOpType
    ACT = mybir.ActivationFunctionType
    P, F, TB, V, R, G, KT, W, BLOCK, EPS = (env[n] for n in ("P", "F", "TB", "V", "R", "G", "KT", "W", "BLOCK", "EPS"))
    x, by_src, ysum, psum, sb = (env[n] for n in ("x", "by_src", "ysum", "psum", "sb"))
    ident, unit, trash, is_real, mask_p, mask_d, neghalf, zeros = (
        env[n] for n in ("ident", "unit", "trash", "is_real", "mask_p", "mask_d", "neghalf", "zeros"))
    w1_sb, w2_sb, wo_sb, b1_sb, b2_sb, wr_sb, wpp_sb, wpd_sb = (
        env[n] for n in ("w1_sb", "w2_sb", "wo_sb", "b1_sb", "b2_sb", "wr_sb", "wpp_sb", "wpd_sb"))
    xg, xn, stats, mv, ve, rstd, hT, s1, s2, h2, s3, urow = (
        env[n] for n in ("xin", "xn", "stats", "mv", "ve", "rstd", "hT", "s1", "s2", "h2", "s3", "rowout"))
    MLP = (2, 3, 1)
    V3 = 3 * V
    U = 3

    er = sb("er", [P, U, TB, W])
    nxt = sb("nxt", [P, U, TB], i32)
    srcf = sb("srcf", [P, U, TB])
    nxtf = sb("nxtf", [P, U, TB])
    ends = sb("ends", [P, U, TB])
    row_f = sb("row_f", [P, U, TB])
    row_i = sb("row_i", [P, U, TB], i32)
    eT = sb("eT", [KT, U, BLOCK])
    eTp = sb("eTp", [V3, U, BLOCK])
    eTd = sb("eTd", [V3, U, BLOCK])
    gate = sb("gate", [P, 3, BLOCK])
    mT = sb("mT", [P, U, 2, BLOCK])
    msg = sb("msg", [P, U, TB, F])
    AB = sb("AB", [P, 2, 4, F])
    same = sb("same", [P, 2, P])
    gram = sb("gram", [P, 2, 2, P])
    last_w = sb("last_w", [P, 2, V3])
    prod = sb("prod", [P, 2, 2, F])
    allsum = sb("allsum", [P, 2, 2, F])

    HT_AT_G, BANK_A, BANK_B, BANK_O, BANK_AB, BANK_SEG, BANK_C, BANK_TU = psum
    SRC_T, GRAM, S_CARRY = BANK_SEG[:, 0:P], BANK_SEG[:, P:3 * P], BANK_SEG[0:V, 3 * P:4 * P]
    BANK_T, BANK_U = BANK_TU[:, 0:2 * F], BANK_TU[:, 3 * F:4 * F]

    def tiles(dram_rows):
        return dram_rows.rearrange("(t r) w -> r t w", r=R)

    with ExitStack() as own:
        def sem(nm):
            return own.enter_context(nc.semaphore("e_" + nm))
        nxt_clear = sem("nxt_cleared")
        rows_in = [sem(f"edge_rows_in{i}") for i in range(U)]
        x_in = [sem(f"gathered{i}") for i in range(U)]
        added = [sem(f"added{i}") for i in range(TB)]
        unit_done, srcf_done, idx_a, idx_b, idx_c, row_done = (sem(s) for s in ("unit_done", "srcf_done", "idx_a", "idx_b", "idx_c", "rows_done"))
        st_done, mv_done, ve_done, rstd_done, norm_done = (sem(s) for s in ("stats_done", "meanvar_done", "vareps_done", "rstd_done", "norm_done"))
        xT_done, hT_done, s1_done, eT_ps, eT_done, eTm_done = (sem(s) for s in ("xT_done", "hT_done", "s1_done", "eT_in_psum", "eT_done", "eT_masked"))
        a_done, s2_done, b_done, h2_done, s3_done, g_ps, gate_done, o_done, msg_done = (
            sem(s) for s in ("a_done", "s2_done", "b_done", "h2_done", "s3_done", "gate_in_psum", "gate_done", "o_done", "msg_done"))
        seg_ps, ab_ps, ab_done, ab_carried, same_done, gram_done, lastw_done, c_done, ms_done = (
            sem(s) for s in ("seg_in_psum", "ab_in_psum", "ab_done", "ab_carried", "same_done", "gram_done", "last_weights_done", "carry_done", "sums_carried"))
        t_done, prod_done, sum1_done, sum_done, u_ps, u_done = (
            sem(s) for s in ("t_done", "prod_done", "sum1_done", "sum_done", "u_in_psum", "u_done"))

        passed = sem("waits_passed")

        def steps(eng, body):
            run_steps(eng, body, U, G, U + 1, 2, 1)

        def nm(k, lag, m, plus=0):
            return k.n(lag) * 3 + (m + plus)

        def nt(k, j, plus=0):
            return k.n(1) * TB + (j + plus)

        def first_tile(k, j, back):
            return k.peeled and (k.c - 1) * TB + j - back < 0

        def previous(k, j):
            return k.live(1 if j else 2)

        with nc.Block() as block:
            @block.sync
            def _(sp):
                sp.wait_ge(nxt_clear, 1)

                def load(k, lag):
                    if not k.live(lag):
                        return
                    s = k.slot(lag)
                    if k.has(lag + U):
                        sp.wait_ge(c_done, k.n(lag + U - 1) * TB)
                        alone(sp, passed)
                        sp.wait_ge(row_done, k.n(lag + U - 1))
                        alone(sp, passed)
                        sp.wait_ge(x_in[s], k.uses(lag + U) * 64)
                        alone(sp, passed)
                    start = k.n(lag) * (TB * R)
                    sp.dma_start(er[V:P, s, :, :], tiles(by_src[bass.ds(start + 1, TB * R), :])).then_inc(rows_in[s], 16)
                    sp.dma_start(er[0:V, s, :, :], tiles(by_src[bass.ds(start, TB * R), :])[0].partition_broadcast(V)).then_inc(rows_in[s], 16)
                    with nc.allow_non_contiguous_dma(reason="one word of each row"):
                        sp.dma_start(nxt[V:P, s, :], tiles(by_src[bass.ds(start + 2, TB * R), 0:1])[:, :, 0].bitcast(i32),
                                     allow_slow_non_contiguous=True).then_inc(rows_in[s], 16)

                def body(k):
                    if k.peeled and k.c == 0:
                        load(k, 0)
                    load(k, -1)
                steps(sp, body)

            @block.gpsimd
            def _(pool):
                nc.gpsimd.memset(nxt[:, :, :], 0).then_inc(nxt_clear, 1)

                def gather(k, lag):
                    if not k.live(lag):
                        return
                    s = k.slot(lag)
                    pool.wait_ge(rows_in[s], k.uses(lag) * 48)
                    alone(pool, passed)
                    nc.gpsimd.tensor_copy(er[0:V, s, :, 2:2 + V3], unit[:, :, :]).then_inc(unit_done, 1)
                    if k.has(lag + U):
                        pool.wait_ge(norm_done, k.n(lag + U - 1))
                        alone(pool, passed)
                    for j in range(TB):
                        nc.gpsimd.indirect_dma_start(
                            out=xg[:, s, j, :], out_offset=None, in_=x,
                            in_offset=bass.IndirectOffsetOnAxis(ap=er[:, s, j, 1:2].bitcast(i32), axis=0)).then_inc(x_in[s], 16)

                def scale(k, lag):
                    if k.live(lag):
                        s = k.slot(lag)
                        pool.wait_ge(mv_done, k.n(lag - 1))
                        alone(pool, passed)
                        nc.gpsimd.tensor_scalar(ve[:, s, :], mv[:, s, :, 1], EPS, None, ALU.add).then_inc(ve_done, 1)
                        pool.wait_ge(ve_done, k.n(lag - 1))
                        nc.gpsimd.tensor_tensor(rstd[:, s, :], ve[:, s, :], neghalf[:, :], ALU.pow).then_inc(rstd_done, 1)

                def add_row(k, j):
                    if previous(k, j):
                        b, s = (j - 1) % TB, k.slot(1 if j else 2)
                        pool.wait_ge(u_done, nt(k, j))
                        if not first_tile(k, j, 2):
                            pool.wait_ge(added[(j - 2) % TB], (k.n(0) if j > 1 else k.n(1)) * 16)
                        alone(pool, passed)
                        nc.gpsimd.indirect_dma_start(
                            out=ysum, out_offset=bass.IndirectOffsetOnAxis(ap=row_i[:, s, b:b + 1], axis=0),
                            in_=urow[:, b, 0, :], in_offset=None, compute_op=ALU.add).then_inc(added[b], 16)

                def body(k):
                    if k.peeled and k.c == 0:
                        gather(k, 0)
                        scale(k, 0)
                    gather(k, -1)
                    if k.live(0):
                        s = k.slot()
                        pool.wait_ge(eT_done, k.n(-1))
                        if k.has(U):
                            pool.wait_ge(seg_ps, k.n(U - 1) * TB)
                        alone(pool, passed)
                        nc.gpsimd.tensor_scalar(eTp[:, s, :], eT[0:V3, s, :], mask_p[0:V3, :], None, ALU.mult)
                        nc.gpsimd.tensor_scalar(eTd[:, s, :], eT[0:V3, s, :], mask_d[0:V3, :], None, ALU.mult).then_inc(eTm_done, 1)
                    for j in range(TB):
                        add_row(k, j)
                        if k.live(1):
                            s = k.slot(1)
                            pool.wait_ge(prod_done, nt(k, j, 1))
                            if not first_tile(k, j, 2):
                                pool.wait_ge(u_ps, nt(k, j, -1))
                            nc.gpsimd.tensor_tensor(allsum[:, j % 2, 0, :], prod[:, j % 2, 0, :], prod[:, j % 2, 1, :], ALU.add).then_inc(sum1_done, 1)
                            pool.wait_ge(sum1_done, nt(k, j, 1))
                            pool.wait_ge(ms_done, nt(k, j, 1))
                            nc.gpsimd.tensor_tensor(allsum[:, j % 2, 1, :], allsum[:, j % 2, 0, :], msg[:, s, j, :], ALU.add).then_inc(sum_done, 1)
                        if j == 1:
                            scale(k, -1)
                steps(pool, body)
                for j in range(TB):
                    pool.wait_ge(added[j], 16 * G)

            @block.vector
            def _(dve):
                def indices(k, lag):
                    if not k.live(lag):
                        return
                    s = k.slot(lag)
                    n = k.n(lag - 1)
                    dve.wait_ge(rows_in[s], k.uses(lag) * 48)
                    if k.has(lag + U):
                        dve.wait_ge(seg_ps, k.n(lag + U - 1) * TB)
                        dve.wait_ge(added[TB - 1], k.n(lag + U - 1) * 16)
                    nc.vector.tensor_copy(srcf[:, s, :], er[:, s, :, 0].bitcast(i32))
                    nc.vector.tensor_copy(nxtf[:, s, :], nxt[:, s, :]).then_inc(srcf_done, 1)
                    dve.wait_ge(srcf_done, n)
                    nc.vector.tensor_tensor(ends[:, s, :], srcf[:, s, :], nxtf[:, s, :], ALU.not_equal)
                    nc.vector.tensor_scalar(row_f[:, s, :], srcf[:, s, :], trash[:, 0:1], is_real[:, 0:1], ALU.subtract, ALU.mult).then_inc(idx_a, 1)
                    dve.wait_ge(idx_a, n)
                    nc.vector.tensor_tensor(nxtf[:, s, :], row_f[:, s, :], ends[:, s, :], ALU.mult).then_inc(idx_b, 1)
                    dve.wait_ge(idx_b, n)
                    nc.vector.tensor_scalar(row_i[:, s, :], nxtf[:, s, :], trash[:, 0:1], None, ALU.add).then_inc(row_done, 1)

                def stats_of(k, lag):
                    if k.live(lag):
                        s = k.slot(lag)
                        dve.wait_ge(x_in[s], k.uses(lag) * 64)
                        for j in range(TB):
                            last = nc.vector.bn_stats(stats[:, s, j, :], xg[:, s, j, :])
                        last.then_inc(st_done, 1)
                        dve.wait_ge(st_done, k.n(lag - 1))
                        alone(dve, passed)
                        for j in range(TB):
                            last = nc.vector.bn_aggr(mv[:, s, j, :], stats[:, s, j, :])
                        last.then_inc(mv_done, 1)

                def normalise(k, lag):
                    if k.live(lag):
                        s = k.slot(lag)
                        dve.wait_ge(rstd_done, k.n(lag - 1))
                        if k.has(lag + U):
                            dve.wait_ge(xT_done, k.n(lag + U - 1))
                        for j in range(TB):
                            last = nc.vector.tensor_scalar(xn[:, s, j, :], xg[:, s, j, :], mv[:, s, j, 0:1],
                                                           rstd[:, s, j:j + 1], ALU.subtract, ALU.mult)
                        last.then_inc(norm_done, 1)

                def residual(k, m):
                    if k.live():
                        dve.wait_ge(b_done, nm(k, 0, m, 1))
                        if k.has(1):
                            dve.wait_ge(s3_done, nm(k, 1, m, 1))
                        nc.vector.scalar_tensor_tensor(out=h2[:, m, :], in0=BANK_B[:, :], scalar=b2_sb[:, MLP[m]:MLP[m] + 1],
                                                       in1=hT[:, 0, :], op0=ALU.add, op1=ALU.add).then_inc(h2_done, 1)

                def message(k, m):
                    if k.live():
                        s = k.slot()
                        dve.wait_ge(o_done, nm(k, 0, m, 1))
                        dve.wait_ge(gate_done, nm(k, 0, m, 1))
                        if k.has(U):
                            dve.wait_ge(ab_ps if m < 2 else sum_done, k.n(U - 1) * TB)
                            if m == 2:
                                dve.wait_ge(c_done, k.n(U - 1) * TB)
                        dest = mT[:, s, m, :] if m < 2 else msg[:, s, :, :].rearrange("p t f -> p (t f)")
                        nc.vector.tensor_tensor(dest, BANK_O[:, :], gate[:, m, :], ALU.mult).then_inc(msg_done, 1)

                def seg_masks(k, j):
                    if k.live(1):
                        s, q = k.slot(1), j % 2
                        dve.wait_ge(seg_ps, nt(k, j, 1))
                        if not first_tile(k, j, 2):
                            dve.wait_ge(u_ps, nt(k, j, -1))
                            dve.wait_ge(t_done, nt(k, j, -1))
                            dve.wait_ge(c_done, nt(k, j, -1))
                        nc.vector.tensor_scalar(same[:, q, :], SRC_T, srcf[:, s, j:j + 1], None, ALU.is_equal).then_inc(same_done, 1)
                        dve.wait_ge(same_done, nt(k, j, 1))
                        nc.vector.tensor_tensor(gram[:, q, :, :], GRAM.rearrange("p (a b) -> p a b", a=2),
                                                same[:, q, :].unsqueeze(1).to_broadcast([P, 2, P]), ALU.mult).then_inc(gram_done, 1)
                        nc.vector.tensor_scalar(last_w[:, q, :], er[:, s, j, 2:2 + V3], same[:, q, P - 1:P], None, ALU.mult).then_inc(lastw_done, 1)

                def seg_carry(k, j):
                    if k.live(1):
                        s = k.slot(1)
                        dve.wait_ge(msg_done, k.n(0) * 3)
                        if first_tile(k, j, 1):
                            nc.vector.tensor_copy(msg[0:V, s, j, :], zeros[0:V, 0:F]).then_inc(ms_done, 1)
                        else:
                            dve.wait_ge(c_done, nt(k, j, 0))
                            nc.vector.tensor_copy(msg[0:V, s, j, :], S_CARRY).then_inc(ms_done, 1)

                def seg_prod(k, j):
                    if k.live(1):
                        q = j % 2
                        dve.wait_ge(t_done, nt(k, j, 1))
                        dve.wait_ge(ab_carried, nt(k, j, 1))
                        if not first_tile(k, j, 2):
                            dve.wait_ge(sum1_done, nt(k, j, -1))
                        nc.vector.tensor_tensor(prod[:, q, :, :], BANK_T.rearrange("p (a b) -> p a b", a=2),
                                                AB[:, q, :, :].rearrange("p (a b) f -> p a b f", b=2)[:, :, 0, :], ALU.mult).then_inc(prod_done, 1)

                def body(k):
                    if k.peeled and k.c == 0:
                        indices(k, 0)
                        stats_of(k, 0)
                        normalise(k, 0)
                    seg_carry(k, 0)
                    if k.live():
                        dve.wait_ge(xT_done, k.n(-1))
                        if k.has(1):
                            dve.wait_ge(s1_done, k.n(0))
                        nc.vector.tensor_scalar_max(hT[:, 0, :], HT_AT_G[:, :], 0.0).then_inc(hT_done, 1)
                    seg_masks(k, 0)
                    indices(k, -1)
                    seg_prod(k, 0)
                    seg_carry(k, 1)
                    seg_masks(k, 1)
                    residual(k, 0)
                    seg_carry(k, 2)
                    seg_prod(k, 1)
                    residual(k, 1)
                    message(k, 0)
                    seg_masks(k, 2)
                    stats_of(k, -1)
                    residual(k, 2)
                    seg_carry(k, 3)
                    seg_prod(k, 2)
                    message(k, 1)
                    normalise(k, -1)
                    seg_masks(k, 3)
                    message(k, 2)
                    seg_prod(k, 3)
                steps(dve, body)

            @block.scalar
            def _(act):
                def silu1(k):
                    if k.live():
                        act.wait_ge(hT_done, k.n(-1))
                        if k.has(1):
                            act.wait_ge(a_done, nm(k, 1, 2, 1))
                        nc.scalar.activation(s1[:, 0, :], hT[:, 0, :], ACT.Silu).then_inc(s1_done, 1)

                def silu2(k, m):
                    if k.live():
                        act.wait_ge(a_done, nm(k, 0, m, 1))
                        if k.has(1):
                            act.wait_ge(b_done, nm(k, 1, m, 1))
                        nc.scalar.activation(s2[:, m, :], BANK_A[:, :], ACT.Silu, bias=b1_sb[:, MLP[m]:MLP[m] + 1]).then_inc(s2_done, 1)

                def silu3(k, m):
                    if k.live():
                        act.wait_ge(h2_done, nm(k, 0, m, 1))
                        if k.has(1):
                            act.wait_ge(o_done, nm(k, 1, m, 1))
                        nc.scalar.activation(s3[:, m, :], h2[:, m, :], ACT.Silu).then_inc(s3_done, 1)

                def edges_T(k):
                    if k.live():
                        act.wait_ge(eT_ps, k.n(-1))
                        if k.has(U):
                            act.wait_ge(seg_ps, k.n(U - 1) * TB)
                        nc.scalar.copy(eT[:, k.slot(), :], HT_AT_G[0:KT, :]).then_inc(eT_done, 1)

                def gates(k, m):
                    if k.live():
                        act.wait_ge(g_ps, nm(k, 0, m, 1))
                        if k.has(1):
                            act.wait_ge(msg_done, nm(k, 1, m, 1))
                        nc.scalar.copy(gate[:, m, :], HT_AT_G[:, :]).then_inc(gate_done, 1)

                def halves(k, j):
                    if k.live(1):
                        q = j % 2
                        act.wait_ge(ab_ps, nt(k, j, 1))
                        if not first_tile(k, j, 2):
                            act.wait_ge(c_done, nt(k, j, -1))
                            act.wait_ge(t_done, nt(k, j, -1))
                            act.wait_ge(prod_done, nt(k, j, -1))
                        flat = AB[:, q, :, :].rearrange("p a f -> p (a f)")
                        nc.scalar.copy(flat, BANK_AB[:, :]).then_inc(ab_done, 1)
                        act.wait_ge(ab_done, nt(k, j, 1))
                        if first_tile(k, j, 1):
                            nc.scalar.copy(flat[0:V, :], zeros[0:V, :]).then_inc(ab_carried, 1)
                        else:
                            act.wait_ge(c_done, nt(k, j, 0))
                            nc.scalar.copy(flat[0:V, :], BANK_C[0:V, :]).then_inc(ab_carried, 1)

                def sums_out(k, j):
                    if previous(k, j):
                        b = (j - 1) % TB
                        act.wait_ge(u_ps, nt(k, j))
                        if not first_tile(k, j, TB + 1):
                            act.wait_ge(added[b], (k.n(1) if j else k.n(2)) * 16)
                        nc.scalar.copy(urow[:, b, 0, :], BANK_U).then_inc(u_done, 1)

                def body(k):
                    halves(k, 0)
                    silu1(k)
                    sums_out(k, 0)
                    edges_T(k)
                    silu2(k, 0)
                    gates(k, 0)
                    silu2(k, 1)
                    halves(k, 1)
                    silu3(k, 0)
                    sums_out(k, 1)
                    silu2(k, 2)
                    gates(k, 1)
                    silu3(k, 1)
                    halves(k, 2)
                    sums_out(k, 2)
                    silu3(k, 2)
                    gates(k, 2)
                    halves(k, 3)
                    sums_out(k, 3)
                steps(act, body)

            @block.tensor
            def _(pe):
                def rows_T(k):
                    if k.live():
                        pe.wait_ge(norm_done, k.n(-1))
                        if k.has(1):
                            pe.wait_ge(gate_done, nm(k, 1, 2, 1))
                        for j in range(TB):
                            last = nc.tensor.transpose(HT_AT_G[:, j * P:(j + 1) * P], xn[:, k.slot(), j, :], ident[:, :])
                        last.then_inc(xT_done, 1)

                def edges_T(k):
                    if k.live():
                        pe.wait_ge(unit_done, k.n(-1))
                        pe.wait_ge(rows_in[k.slot()], k.uses() * 48)
                        pe.wait_ge(hT_done, k.n(-1))
                        alone(pe, passed)
                        for j in range(TB):
                            last = nc.tensor.transpose(HT_AT_G[0:KT, j * P:(j + 1) * P], er[:, k.slot(), j, 2:W], ident[:, :])
                        last.then_inc(eT_ps, 1)

                def up(k, m):
                    if k.live():
                        pe.wait_ge(s1_done, k.n(-1))
                        if m or k.has(1):
                            pe.wait_ge(s2_done, nm(k, 0, m, 0))
                        nc.tensor.matmul(BANK_A[:, :], w1_sb[:, MLP[m], :], s1[:, 0, :], start=True, stop=True).then_inc(a_done, 1)

                def down(k, m):
                    if k.live():
                        pe.wait_ge(s2_done, nm(k, 0, m, 1))
                        if m or k.has(1):
                            pe.wait_ge(h2_done, nm(k, 0, m, 0))
                        nc.tensor.matmul(BANK_B[:, :], w2_sb[:, MLP[m], :], s2[:, m, :], start=True, stop=True).then_inc(b_done, 1)

                def gates(k, m):
                    if k.live():
                        pe.wait_ge(eT_done, k.n(-1))
                        if m:
                            pe.wait_ge(gate_done, nm(k, 0, m, 0))
                        if m < 2:
                            last = nc.tensor.matmul(HT_AT_G[:, :], wr_sb[:, m, :], eT[:, k.slot(), :], start=True, stop=True)
                        else:
                            for j in range(TB):
                                last = nc.tensor.matmul(HT_AT_G[:, j * P:(j + 1) * P], eT[:, k.slot(), j * P:(j + 1) * P], wr_sb[:, m, :], start=True, stop=True)
                        last.then_inc(g_ps, 1)

                def outp(k, m):
                    if k.live():
                        pe.wait_ge(s3_done, nm(k, 0, m, 1))
                        if m or k.has(1):
                            pe.wait_ge(msg_done, nm(k, 0, m, 0))
                        if m < 2:
                            last = nc.tensor.matmul(BANK_O[:, :], wo_sb[:, MLP[m], :], s3[:, m, :], start=True, stop=True)
                        else:
                            for j in range(TB):
                                last = nc.tensor.matmul(BANK_O[:, j * P:(j + 1) * P], s3[:, m, j * P:(j + 1) * P], wo_sb[:, MLP[m], :], start=True, stop=True)
                        last.then_inc(o_done, 1)

                def seg(k, j):
                    if k.live(1):
                        s, cols = k.slot(1), slice(j * P, (j + 1) * P)
                        pe.wait_ge(eTm_done, k.n(0))
                        pe.wait_ge(row_done, k.n(0))
                        if not first_tile(k, j, 1):
                            pe.wait_ge(gram_done, nt(k, j))
                        pe.wait_ge(ms_done, nt(k, j, 1))
                        nc.tensor.transpose(SRC_T, srcf[:, s, j:j + 1].to_broadcast([P, P]), ident[:, :])
                        nc.tensor.matmul(GRAM[:, 0:P], eTp[:, s, cols], eT[0:V3, s, cols], start=True, stop=True)
                        nc.tensor.matmul(GRAM[:, P:2 * P], eTd[:, s, cols], eT[0:V3, s, cols], start=True, stop=True).then_inc(seg_ps, 1)

                def halves(k, j):
                    if k.live(1):
                        s, cols = k.slot(1), slice(j * P, (j + 1) * P)
                        pe.wait_ge(msg_done, nm(k, 1, 1, 1))
                        if not first_tile(k, j, 1):
                            pe.wait_ge(ab_done, nt(k, j, 0))
                        nc.tensor.matmul(BANK_AB[:, 0:2 * F], mT[:, s, 0, cols], wpp_sb[:, :], start=True, stop=True)
                        nc.tensor.matmul(BANK_AB[:, 2 * F:4 * F], mT[:, s, 1, cols], wpd_sb[:, :], start=True, stop=True).then_inc(ab_ps, 1)

                def carry(k, j):
                    if k.live(1):
                        s, q = k.slot(1), j % 2
                        pe.wait_ge(lastw_done, nt(k, j, 1))
                        pe.wait_ge(ab_carried, nt(k, j, 1))
                        pe.wait_ge(ms_done, nt(k, j, 1))
                        flat = AB[:, q, :, :].rearrange("p a f -> p (a f)")
                        nc.tensor.matmul(BANK_C[0:V, 0:2 * F], last_w[:, q, V:2 * V], flat[:, 0:2 * F], start=True, stop=True)
                        nc.tensor.matmul(BANK_C[0:V, 2 * F:4 * F], last_w[:, q, 2 * V:V3], flat[:, 2 * F:4 * F], start=True, stop=True)
                        nc.tensor.matmul(S_CARRY, last_w[:, q, 0:V], msg[:, s, j, :], start=True, stop=True).then_inc(c_done, 1)

                def inner(k, j):
                    if k.live(1):
                        q = j % 2
                        pe.wait_ge(gram_done, nt(k, j, 1))
                        if not first_tile(k, j, 1):
                            pe.wait_ge(u_done, nt(k, j))
                        nc.tensor.matmul(BANK_T[:, 0:F], gram[:, q, 0, :], AB[:, q, 1, :], start=True, stop=True)
                        nc.tensor.matmul(BANK_T[:, F:2 * F], gram[:, q, 1, :], AB[:, q, 3, :], start=True, stop=True).then_inc(t_done, 1)

                def sums(k, j):
                    if previous(k, j):
                        q = (j - 1) % 2
                        pe.wait_ge(sum_done, nt(k, j))
                        nc.tensor.matmul(BANK_U, same[:, q, :], allsum[:, q, 1, :], start=True, stop=True).then_inc(u_ps, 1)

                def body(k):
                    rows_T(k)
                    seg(k, 0)
                    halves(k, 0)
                    sums(k, 0)
                    edges_T(k)
                    up(k, 0)
                    carry(k, 0)
                    inner(k, 0)
                    gates(k, 0)
                    up(k, 1)
                    seg(k, 1)
                    halves(k, 1)
                    down(k, 0)
                    sums(k, 1)
                    up(k, 2)
                    carry(k, 1)
                    inner(k, 1)
                    gates(k, 1)
                    down(k, 1)
                    outp(k, 0)
                    seg(k, 2)
                    halves(k, 2)
                    sums(k, 2)
                    down(k, 2)
                    carry(k, 2)
                    inner(k, 2)
                    outp(k, 1)
                    gates(k, 2)
                    seg(k, 3)
                    halves(k, 3)
                    sums(k, 3)
                    outp(k, 2)
                    carry(k, 3)
                    inner(k, 3)
                steps(pe, body)


_PRE = "L0_gnn_"
_INS = ["x", "src", "dst", "edge_attr_3", "edge_attr_32", "edge_attr_5"] + [
    _PRE + n for n in ("w_rs", "w_rp", "w_rd", "w_pp", "w_pd", "res_w1", "res_b1", "res_w2", "res_b2", "res_wout")]


def kernel(**inputs):
    import numpy as _np
    import concourse.bacc as _bacc
    from concourse import mybir as _mybir
    from concourse.bass_utils import run_bass_kernel_spmd as _run

    nc = _bacc.Bacc("TRN2", target_bir_lowering=False, num_devices=1)
    arrays, args = {}, []
    for name in _INS:
        a = _np.ascontiguousarray(inputs[name])
        arrays[f"in_{name}_dram"] = a
        args.append(nc.dram_tensor(f"in_{name}_dram", a.shape, _mybir.dt.from_np(a.dtype), kind="ExternalInput").ap())
    out = nc.dram_tensor("out_0_dram", inputs["x"].shape, _mybir.dt.float32, kind="ExternalOutput").ap()
    gnn_kernel(nc, *args, out)
    r = _run(nc, [arrays], core_ids=[0])
    return r.results[0]["out_0_dram"]
```

```python
import concourse.bass as bass
from concourse import mybir
from contextlib import ExitStack


class Step:

    def __init__(self, i, c, unroll, total):
        if isinstance(i, int):
            i, c = 0, i * unroll + c
        self.i, self.c, self.unroll, self.total = i, c, unroll, total
        self.peeled = isinstance(i, int)
        self.part = self.done = self.place = None

    def live(self, lag=0):
        return not self.peeled or 0 <= self.c - lag < self.total

    def has(self, lag):
        return not self.peeled or self.c - lag >= 0

    def n(self, lag=0):
        return self.i * self.unroll + (self.c - lag)

    def slot(self, lag=0):
        return (self.c - lag) % self.unroll

    def uses(self, lag=0):
        return self.i + (self.c - lag) // self.unroll + 1


def alone(eng, passed):
    eng.sem_inc(passed, 1)


def run_steps(eng, body, unroll, total, first, last_lag, ahead, parts=(), beside=None):
    begin = -(-first // unroll)
    end = (total - ahead) // unroll
    for c in range(begin * unroll):
        body(Step(0, c, unroll, total))
    left = end - begin - sum(parts)
    for n, count in enumerate([*parts, left] if left else parts):
        if beside:
            beside.before(n)
        with eng.Fori(begin, begin + count) as i:
            for c in range(unroll):
                step = Step(i, c, unroll, total)
                step.part, step.done, step.place = n, i - begin, c
                body(step)
        begin += count
    for c in range(end * unroll, total + last_lag):
        body(Step(0, c, unroll, total))


class Beside:

    def __init__(self, passes, picks, before, during=None):
        self.passes, self.picks, self.before, self.during = passes, picks, before, during

    def __call__(self, k, j):
        if k.part in self.passes and j < self.picks[k.place]:
            self.during(k, j)


def load_group(eng, by_src, er, nxt, s, start, V, R, TB, done):
    def tiles(dram_rows):
        return dram_rows.rearrange("(t r) w -> r t w", r=R)

    P = er.shape[0]
    eng.dma_start(er[V:P, s, :, :], tiles(by_src[bass.ds(start + 1, TB * R), :])).then_inc(done, 16)
    eng.dma_start(er[0:V, s, :, :], tiles(by_src[bass.ds(start, TB * R), :])[0].partition_broadcast(V)).then_inc(done, 16)
    eng.dma_start(nxt[V:P, s, :], tiles(by_src[bass.ds(start + 2, TB * R), 0:1])[:, :, 0].bitcast(mybir.dt.int32),
                  allow_slow_non_contiguous=True).then_inc(done, 16)


def gather_tile(pool, x, xg, er, s, j, done):
    pool.indirect_dma_start(
        out=xg[:, s, j, :], out_offset=None, in_=x,
        in_offset=bass.IndirectOffsetOnAxis(ap=er[:, s, j, 1:2].bitcast(mybir.dt.int32), axis=0)).then_inc(done, 16)


def gnn_kernel(nc, x, src, dst, attr3, attr32, attr5, w_rs, w_rp, w_rd, w_pp, w_pd,
               w1, b1, w2, b2, wout, out):
    fp32, i32, bf16 = mybir.dt.float32, mybir.dt.int32, mybir.dt.bfloat16
    ALU = mybir.AluOpType
    ACT = mybir.ActivationFunctionType

    P = 128
    N, F = x.shape
    E = src.shape[0]
    NRBF, NP3, ND5, NMLP = attr32.shape[1], attr3.shape[1], attr5.shape[1], w1.shape[0]
    EPS = 1e-5

    TB = 4
    BLOCK = TB * P
    NB = -(-N // BLOCK)

    PICKS = (3, 2, 3, 2)
    PER = sum(PICKS)
    SORT_ITERATIONS = -(-E // (P * PER))
    T = SORT_ITERATIONS * PER
    SORT_PARTS = [1, SORT_ITERATIONS - 1, 1, SORT_ITERATIONS]
    BURST = 2 * PER
    FULL_P = E // T
    assert T <= 256
    REST = E - FULL_P * T

    V = 5
    R = P - V
    G = -(-(-(-E // R)) // TB)
    ROWS = G * TB * R
    C_P, C_ONE, C_RBF_A, C_D = 0, V, 2 * V, 32
    C_RBF_B = C_D + V
    NRBF_A = C_D - C_RBF_A
    KT = C_RBF_B + NRBF - NRBF_A
    W = 2 + KT
    SRC_ROWS = max(ROWS + 2, P * T + 1)
    PAD = N
    LOW = 256

    xb_view = lambda row, dram: dram[row, :].rearrange("(p t) f -> p t f", t=TB)

    ctx = ExitStack()
    with ctx:
        def sb(name, shape, dt=fp32):
            return ctx.enter_context(nc.sbuf_tensor(name, shape, dt))

        def sem(name):
            return ctx.enter_context(nc.semaphore(name))

        by_low = nc.dram_tensor("edges_by_low", [P * T, W], fp32, kind="Internal").ap()
        by_src = nc.dram_tensor("edges_by_src", [SRC_ROWS, W], fp32, kind="Internal").ap()
        ysum = nc.dram_tensor("node_sums", [N + P, F], fp32, kind="Internal").ap()

        ident = sb("ident", [P, P])
        ident_h = sb("ident_h", [P, P], bf16)
        before_h = sb("before_h", [P, P], bf16)
        ones_h = sb("ones_h", [P, P], bf16)
        digits_h = sb("digits_h", [P, LOW], bf16)
        column = sb("column", [P, LOW])
        part = sb("part", [P, 1])
        trash = sb("trash", [P, 1])
        is_real = sb("is_real", [P, 1])
        neghalf = sb("neghalf", [P, TB])
        unit = sb("unit", [V, TB, KT])
        w1_sb = sb("w1_sb", [P, NMLP, F])
        w2_sb = sb("w2_sb", [P, NMLP, F])
        wo_sb = sb("wo_sb", [P, NMLP, F])
        b1_sb = sb("b1_sb", [P, NMLP])
        b2_sb = sb("b2_sb", [P, NMLP])
        wr_sb = sb("wr_sb", [KT, 3, F])
        wpp_sb = sb("wpp_sb", [P, 2 * F])
        wpd_sb = sb("wpd_sb", [P, 2 * F])
        zeros = sb("zeros", [P, 4 * F])

        psum = [ctx.enter_context(nc.psum_tensor(f"bank{i}", [P, 512], fp32)) for i in range(8)]

        xin = sb("xin", [P, 4, TB, F])
        yin = sb("yin", [P, 4, TB, F])
        xn = sb("xn", [P, 4, TB, F])
        stats = sb("stats", [P, 4, TB, 6])
        mv = sb("mv", [P, 4, TB, 2])
        ve = sb("ve", [P, 4, TB])
        rstd = sb("rstd", [P, 4, TB])
        hT = sb("hT", [P, 4, BLOCK])
        s1 = sb("s1", [P, 4, BLOCK])
        s2 = sb("s2", [P, 4, BLOCK])
        h2 = sb("h2", [P, 4, BLOCK])
        s3 = sb("s3", [P, 4, BLOCK])
        rowout = sb("rowout", [P, 4, TB, F])

        U = 3
        er = sb("er", [P, U, TB, W])
        nxt = sb("nxt", [P, U, TB], i32)
        rows_in = [sem(f"edge_rows_in{i}") for i in range(U)]
        gathered = [sem(f"gathered{i}") for i in range(U)]
        unit_done = sem("carry_rows_set")

        own = ctx.enter_context(ExitStack())

        def psb(name, shape, dt=fp32):
            return own.enter_context(nc.sbuf_tensor(name, shape, dt))

        def psem(name):
            return own.enter_context(nc.semaphore(name))

        pay = psb("pay", [P, T, W])
        st_src = psb("st_src", [P, T], i32)
        st_dst = psb("st_dst", [P, T], i32)
        st3 = psb("st3", [P, T, NP3])
        st5 = psb("st5", [P, T, ND5])
        st32 = psb("st32", [P, T, NRBF])
        digit_i = psb("digit_i", [P, T], i32)
        digit_f = psb("digit_f", [P, T])
        onehot = psb("onehot", [P, T + 1, LOW], bf16)
        counts_h = psb("counts_h", [P, LOW], bf16)
        total = psb("total", [P, LOW])
        upto = psb("upto", [P, LOW])
        base = psb("base", [P, LOW])
        picked = psb("picked", [P, 2, LOW])
        rank_f = psb("rank_f", [P, 2])
        rank_i = psb("rank_i", [P, PER], i32)
        leaving = psb("leaving", [P, PER, W])
        padrow = psb("padrow", [P, 3, W])
        leadrow = psb("leadrow", [1, W])

        s_w = psem("weights_in")
        s_w2 = psem("edge_weights_in")
        s_cst = psem("constants_made")
        s_staged = psem("stages_cleared")
        s_edges = psem("edges_in")
        s_pay = psem("payload_made")
        s_init = psem("tables_initialised")
        s_dig = psem("digits_made")
        s_alone = psem("pool_waits_passed")
        s_oh = psem("onehots_made")
        s_cnt = psem("counts_done")
        s_counts = psem("counts_read")
        s_dve = psem("dve_chain")
        s_base = psem("bases_made")
        s_seed = psem("bases_added")
        s_pick = psem("ranks_picked")
        s_rank = psem("rank_indices_made")
        s_scat = [psem(f"scattered{i}") for i in range(PER)]
        s_back = psem("sorted_by_low_in")
        s_leave = psem("tiles_leaving")

        groups = []
        at = P * T + 1
        left = max(SRC_ROWS - at, 0)
        while left:
            each = 3 if left >= 3 else 1
            parts = min(P, left // each)
            groups.append((at, parts, each))
            at += parts * each
            left -= parts * each

        def load_parts(dram, tile, eng, s, per):
            n = 0
            cut = FULL_P // 16 * 16
            flat = dram.rearrange("e c -> (e c)") if len(dram.shape) == 2 else dram
            for lo, hi, size in ((0, cut, T), (cut, FULL_P, T), (FULL_P, FULL_P + 1, REST)):
                if hi > lo and size:
                    first = lo * T * per
                    eng.dma_start(tile[lo:hi, 0:size * per],
                                  flat[first:first + (hi - lo) * size * per].rearrange("(p c) -> p c", p=hi - lo)).then_inc(s, 16)
                    n += 1
            return n

        n_edge_loads = [0]

        def load_weights(sp):
            sp.dma_start(w1_sb[:, :, :], w1.rearrange("m k n -> k m n")).then_inc(s_w, 16)
            sp.dma_start(w2_sb[:, :, :], w2.rearrange("m k n -> k m n")).then_inc(s_w, 16)
            sp.dma_start(wo_sb[:, :, :], wout.rearrange("m k n -> k m n")).then_inc(s_w, 16)
            with nc.allow_non_contiguous_dma(reason="biases to partitions"):
                sp.dma_start(b1_sb[:, :], b1.rearrange("m k -> k m"), allow_slow_non_contiguous=True).then_inc(s_w, 16)
                sp.dma_start(b2_sb[:, :], b2.rearrange("m k -> k m"), allow_slow_non_contiguous=True).then_inc(s_w, 16)

        def make_constants(pool):
            nc.gpsimd.iota(column[:, :], [[1, LOW]], base=0, channel_multiplier=0,
                           allow_small_or_imprecise_dtypes=True)
            nc.gpsimd.iota(part[:, :], [[0, 1]], base=0, channel_multiplier=1,
                           allow_small_or_imprecise_dtypes=True)
            nc.gpsimd.memset(neghalf[:, :], -0.5)
            nc.gpsimd.memset(zeros[:, :], 0.0).then_inc(s_cst, 1)

        def clear_stages(pool, step):
            if step == -1:
                nc.gpsimd.memset(st_src[:, :], PAD)
                nc.gpsimd.memset(st_dst[:, :], 0)
                nc.gpsimd.memset(st3[:, :, :], 0.0)
                nc.gpsimd.memset(st32[:, :, :], 0.0)
            if step == 0:
                nc.gpsimd.memset(st5[:, :, :], 0.0)
                nc.gpsimd.memset(padrow[:, :, :], 0.0)
                nc.gpsimd.memset(nxt[:, :, :], 0)
                nc.gpsimd.memset(leadrow[:, :], 0.0)
                nc.gpsimd.memset(wr_sb[:, :, :], 0.0).then_inc(s_cst, 1)
            if step == 1:
                pool.wait_ge(s_cst, 2)
                nc.gpsimd.memset(padrow[:, :, 0:1].bitcast(i32), PAD)
                nc.gpsimd.memset(leadrow[:, 0:1].bitcast(i32), PAD + 1).then_inc(s_staged, 1)
            if step in (2, 3):
                half = T // 2 * (step - 2)
                nc.gpsimd.memset(pay[:, half:half + T - T // 2, :], 0.0)
            if step == 4:
                nc.gpsimd.memset(ones_h[:, :], 1.0)
                nc.gpsimd.memset(onehot[:, T:T + 1, :], 0.0).then_inc(s_cst, 1)

        def derive_constants(dve):
            n_chain = [0]

            def link(ins):
                n_chain[0] += 1
                ins.then_inc(s_dve, 1)
                dve.wait_ge(s_dve, n_chain[0])

            dve.wait_ge(s_cst, 1)
            nc.vector.tensor_copy(digits_h[:, :], column[:, :])
            nc.vector.tensor_scalar(ident_h[:, :], column[:, 0:P], part[:, 0:1], None, ALU.is_equal)
            nc.vector.tensor_scalar(before_h[:, :], column[:, 0:P], part[:, 0:1], None, ALU.is_gt)
            nc.vector.tensor_scalar(trash[:, :], part[:, :], float(N), None, ALU.add)
            nc.vector.tensor_scalar(is_real[:, :], part[:, :], float(V), None, ALU.is_ge)
            link(nc.vector.tensor_scalar(ident[:, :], column[:, 0:P], part[:, 0:1], None, ALU.is_equal))
            link(nc.vector.memset(unit[:, :, :], 0.0))
            for t in range(TB):
                nc.vector.memset(unit[:, t, C_ONE:C_ONE + 1], 1.0)
                nc.vector.tensor_copy(unit[:, t, C_P:C_P + NP3], ident[0:V, 0:NP3])
                last = nc.vector.tensor_copy(unit[:, t, C_D:C_D + ND5], ident[0:V, 0:ND5])
            link(last)

        class Sort:

            def __init__(self):
                self.passes = {0: (0, 0), 1: (0, 1), 3: (1, 0)}
                self.n_chain = 0
                self.sync = Beside(self.passes, PICKS, self.sync_before)
                self.gpsimd = Beside(self.passes, PICKS, self.gpsimd_before, self.gpsimd_during)
                self.scalar = Beside(self.passes, PICKS, self.scalar_before, self.scalar_during)
                self.vector = Beside(self.passes, PICKS, self.vector_before, self.vector_during)
                self.tensor = Beside(self.passes, PICKS, self.tensor_before, self.tensor_during)

            def at(self, k, j):
                n, done = self.passes[k.part]
                return n, k.done + done, sum(PICKS[:k.place]) + j

            def load_edges(self, n):
                nc.sync.wait_ge(s_staged, 1)
                dram, tile, per = ((attr32, st32, NRBF), (src, st_src, 1), (dst, st_dst, 1), (attr3, st3, NP3), (attr5, st5, ND5))[n]
                flat = tile[:, :] if per == 1 else tile[:, :, :].rearrange("p t c -> p (t c)")
                n_edge_loads[0] += load_parts(dram, flat, nc.sync, s_edges, per)

            def load_late(self):
                nc.sync.dma_start(wpp_sb[:, :], w_pp).then_inc(s_w2, 16)
                nc.sync.dma_start(wpd_sb[:, :], w_pd).then_inc(s_w2, 16)
                nc.sync.dma_start(wr_sb[C_RBF_A:C_D, 0, :], w_rp[0:NRBF_A, :]).then_inc(s_w2, 16)
                nc.sync.dma_start(wr_sb[C_RBF_B:KT, 0, :], w_rp[NRBF_A:NRBF, :]).then_inc(s_w2, 16)
                nc.sync.dma_start(wr_sb[C_RBF_A:C_D, 1, :], w_rd[0:NRBF_A, :]).then_inc(s_w2, 16)
                nc.sync.dma_start(wr_sb[C_RBF_B:KT, 1, :], w_rd[NRBF_A:NRBF, :]).then_inc(s_w2, 16)
                nc.sync.dma_start(wr_sb[C_RBF_A:C_D, 2, :], w_rs[0:NRBF_A, :]).then_inc(s_w2, 16)
                nc.sync.dma_start(wr_sb[C_RBF_B:KT, 2, :], w_rs[NRBF_A:NRBF, :]).then_inc(s_w2, 16)
                nc.sync.dma_start(by_src[0:1, :], leadrow[:, :]).then_inc(s_init, 16)
                for row, parts, each in groups:
                    nc.sync.dma_start(by_src[row:row + parts * each, :].rearrange("(p t) w -> p t w", t=each),
                                 padrow[0:parts, 0:each, :]).then_inc(s_init, 16)
                nc.sync.dma_start(ysum[N:N + P, :], zeros[:, 0:F]).then_inc(s_init, 16)

            def sync_before(self, part):
                if part == 0:
                    self.load_late()

            def scalar_before(self, part):
                if part == 0:
                    act = nc.scalar
                    act.wait_ge(s_cst, 3)
                    act.wait_ge(s_edges, 16 * n_edge_loads[0])
                    nc.scalar.copy(pay[:, :, 2 + C_P:2 + C_P + NP3], st3[:, :, :])
                    nc.scalar.copy(pay[:, :, 2 + C_D:2 + C_D + ND5], st5[:, :, :])
                    nc.scalar.copy(pay[:, :, 2 + C_RBF_A:2 + C_D], st32[:, :, 0:NRBF_A])
                    nc.scalar.copy(pay[:, :, 2 + C_RBF_B:W], st32[:, :, NRBF_A:NRBF]).then_inc(s_pay, 1)
                    act.wait_ge(s_pay, 2)

                if part == 3:
                    nc.scalar.wait_ge(s_back, 16)

            def scalar_during(self, k, j):
                n, i, slot = self.at(k, j)
                act = nc.scalar
                if k.part:
                    act.wait_ge(s_scat[slot], (i + n * SORT_ITERATIONS) * 16)
                nc.scalar.copy(leaving[:, slot, :], pay[:, i * PER + slot, :]).then_inc(s_leave, 1)

            def gpsimd_before(self, part):
                if part == 2:
                    for s in s_scat:
                        nc.gpsimd.wait_ge(s, 16 * SORT_ITERATIONS)
                    nc.gpsimd.dma_start(pay[:, :, :], by_low.rearrange("(p t) w -> p t w", t=T)).then_inc(s_back, 16)
                if part == 3:
                    nc.gpsimd.wait_ge(s_init, 16 * (2 + len(groups)))

            def gpsimd_during(self, k, j):
                n, i, slot = self.at(k, j)
                t = i * PER + slot
                nc.gpsimd.wait_ge(s_rank, t + (n * T + 1))
                alone(nc.gpsimd, s_alone)
                nc.gpsimd.wait_ge(s_leave, t + (n * T + 1))
                alone(nc.gpsimd, s_alone)
                nc.gpsimd.indirect_dma_start(
                    out=(by_low, by_src)[n],
                    out_offset=bass.IndirectOffsetOnAxis(ap=rank_i[:, slot:slot + 1], axis=0),
                    in_=leaving[:, slot, :], in_offset=None).then_inc(s_scat[slot], 16)

            def finish(self, pool):
                for s in s_scat:
                    pool.wait_ge(s, 2 * 16 * SORT_ITERATIONS)
                pool.wait_ge(rows_in[0], 48)
                nc.gpsimd.tensor_copy(er[0:V, 0, :, 2:W], unit[:, :, :]).then_inc(unit_done, 1)
                for j in range(TB):
                    gather_tile(nc.gpsimd, x, yin, er, 0, j, gathered[0])

            def load_first_group(self):
                for s in s_scat:
                    nc.sync.wait_ge(s, 2 * 16 * SORT_ITERATIONS)
                nc.sync.wait_ge(s_init, 16 * (2 + len(groups)))
                with nc.allow_non_contiguous_dma(reason="one word of each row"):
                    load_group(nc.sync, by_src, er, nxt, 0, 0, V, R, TB, rows_in[0])

            def link(self, ins):
                self.n_chain += 1
                ins.then_inc(s_dig, 1)
                nc.vector.wait_ge(s_dig, self.n_chain)

            def vector_before(self, part):
                if part not in (0, 3):
                    return
                n, dve = self.passes[part][0], nc.vector
                if n == 0:
                    dve.wait_ge(s_cst, 3)
                    dve.wait_ge(s_edges, 16 * n_edge_loads[0])
                    nc.vector.memset(pay[:, :, 2 + C_ONE:3 + C_ONE], 1.0)
                    nc.vector.tensor_copy(pay[:, :, 0:1].bitcast(i32), st_src[:, :].unsqueeze(2))
                    nc.vector.tensor_copy(pay[:, :, 1:2].bitcast(i32), st_dst[:, :].unsqueeze(2)).then_inc(s_pay, 1)
                    self.link(nc.vector.tensor_single_scalar(digit_i[:, :], st_src[:, :], LOW - 1, op=ALU.bitwise_and))
                else:
                    dve.wait_ge(s_back, 16)
                    self.link(nc.vector.tensor_single_scalar(digit_i[:, :], pay[:, :, 0].bitcast(i32), LOW.bit_length() - 1,
                                                        op=ALU.arith_shift_right))
                self.link(nc.vector.tensor_copy(digit_f[:, :], digit_i[:, :]))
                with dve.Fori(0, T // BURST) as i:
                    for c in range(BURST):
                        t = i * BURST + c
                        last = nc.vector.tensor_scalar(onehot[:, t, :], digits_h[:, :], digit_f[:, bass.ds(t, 1)], None, ALU.is_equal)
                    last.then_inc(s_oh, 1)
                dve.wait_ge(s_cnt, 2 * n + 1)
                nc.vector.tensor_copy(counts_h[:, :], psum[6][:, 0:LOW]).then_inc(s_counts, 1)
                dve.wait_ge(s_cnt, 2 * n + 2)
                self.link(nc.vector.tensor_copy(total[:, :], psum[6][:, 0:LOW]))
                self.link(nc.vector.tensor_tensor_scan(upto[:, :], total[:, :], zeros[:, 0:LOW], 0.0, ALU.add, ALU.add))
                nc.vector.tensor_tensor(base[:, :], upto[:, :], total[:, :], ALU.subtract).then_inc(s_base, 1)

            def vector_during(self, k, j):
                n, i, slot = self.at(k, j)
                dve = nc.vector
                t, q = i * PER + slot, slot % 2
                dve.wait_ge(s_seed, t + (n * (T + 2) + 1))
                nc.vector.scalar_tensor_tensor(
                    out=picked[:, q, :], in0=psum[4 + q][:, 0:LOW], scalar=1.0, in1=onehot[:, t, :],
                    op0=ALU.mult, op1=ALU.mult, accum_out=rank_f[:, q:q + 1]).then_inc(s_pick, 1)

            def ranks(self, k, j):
                if k.part not in self.passes or j >= PICKS[k.place]:
                    return
                n, i, slot = self.at(k, j)
                t, q, dve = i * PER + slot, slot % 2, nc.vector
                dve.wait_ge(s_pick, t + (n * T + 1))
                if k.part:
                    dve.wait_ge(s_scat[slot], (i + n * SORT_ITERATIONS) * 16)
                nc.vector.tensor_scalar(rank_i[:, slot:slot + 1], rank_f[:, q:q + 1], float(n), None, ALU.add).then_inc(s_rank, 1)

            def tensor_before(self, part):
                if part not in (0, 3):
                    return
                n, pe = self.passes[part][0], nc.tensor
                start = dict(stop=True, skip_group_check=True)

                def count(t, first):
                    return nc.tensor.matmul(psum[6][:, 0:LOW], ident_h[:, :], onehot[:, t, :], start=first, **start)
                pe.wait_ge(s_oh, n * (T // BURST) + 1)
                for t in range(BURST):
                    count(t, t == 0)
                with pe.Fori(1, T // BURST - 1) as i:
                    pe.wait_ge(s_oh, i + (n * (T // BURST) + 1))
                    for c in range(BURST):
                        count(i * BURST + c, False)
                pe.wait_ge(s_oh, (n + 1) * (T // BURST))
                for t in range(T - BURST, T):
                    last = count(t, False)
                last.then_inc(s_cnt, 1)
                pe.wait_ge(s_counts, n + 1)
                for bank, lhsT in ((4, before_h), (5, before_h), (6, ones_h)):
                    last = nc.tensor.matmul(psum[bank][:, 0:LOW], lhsT[:, :], counts_h[:, :], start=True, **start)
                last.then_inc(s_cnt, 1)
                pe.wait_ge(s_base, n + 1)
                nc.tensor.matmul(psum[4][:, 0:LOW], ident[:, :], base[:, :], start=False, **start).then_inc(s_seed, 1)
                nc.tensor.matmul(psum[5][:, 0:LOW], ident[:, :], base[:, :], start=False, **start)
                nc.tensor.matmul(psum[5][:, 0:LOW], ident_h[:, :], onehot[:, 0, :], start=False, **start).then_inc(s_seed, 1)

            def tensor_during(self, k, j):
                n, i, slot = self.at(k, j)
                pe = nc.tensor
                t, q = i * PER + slot, slot % 2
                pe.wait_ge(s_pick, t + (n * T + 1))
                nc.tensor.matmul(psum[4 + q][:, 0:LOW], ident_h[:, :], onehot[:, t, :], start=False, stop=True, skip_group_check=True)
                nc.tensor.matmul(psum[4 + q][:, 0:LOW], ident_h[:, :], onehot[:, t + 1, :], start=False, stop=True,
                                 skip_group_check=True).then_inc(s_seed, 1)

        def rows_of(k):
            def at(lag):
                if k.peeled and k.c - lag == NB - 1:
                    return bass.ds(N - BLOCK, BLOCK)
                return bass.ds(k.n(lag) * BLOCK, BLOCK)
            return at

        def wait_stored(eng, stored):
            for b in range(NB - 4, NB):
                eng.wait_ge(stored[b % 4], 16 * (b // 4 + 1))

        def node_phase(final, sort=None):
            m = NMLP - 1 if final else 0
            name = "f_" if final else "n_"
            LAG = 4
            AHEAD = 4
            with ExitStack() as own:
                if not final:
                    own = ctx

                def psem(nm):
                    return own.enter_context(nc.semaphore(name + nm))
                x_in = [psem(f"x_in{i}") for i in range(4)]
                y_in = [psem(f"y_in{i}") for i in range(4)]
                stored = [psem(f"stored{i}") for i in range(4)]
                st_done, mv_done, ve_done, rstd_done, norm_done = (psem(s) for s in ("stats_done", "meanvar_done", "vareps_done", "rstd_done", "norm_done"))
                xT_done, hT_done, s1_done, a_done, s2_done = (psem(s) for s in ("xT_done", "hT_done", "s1_done", "a_done", "s2_done"))
                b_done, h2_done, s3_done, o_done, row_done = (psem(s) for s in ("b_done", "h2_done", "s3_done", "o_done", "row_done"))

                passed = psem("waits_passed")

                def steps(eng, body, between=None):
                    run_steps(eng, body, 4, NB, LAG + 4, LAG, AHEAD, SORT_PARTS if sort else [], between)

                with nc.Block() as block:
                    def store(eng, k):
                        if k.live(LAG):
                            s = k.slot(LAG)
                            eng.wait_ge(row_done, k.n(LAG - 1))
                            alone(eng, passed)
                            if k.peeled and k.c - LAG == NB - 1:
                                for lag in range(1, 4):
                                    eng.wait_ge(stored[k.slot(LAG + lag)], k.uses(LAG + lag) * 16)
                            eng.dma_start(xb_view(rows_of(k)(LAG), out if final else ysum), rowout[:, s, :, :]).then_inc(stored[s], 16)

                    @block.sync
                    def _(sp):
                        def load_x(k, lag):
                            if k.live(lag):
                                at, s = rows_of(k)(lag), k.slot(lag)
                                if k.has(lag + 4):
                                    sp.wait_ge(row_done if final else norm_done, k.n(lag + 3))
                                    alone(sp, passed)
                                sp.dma_start(xin[:, s, :, :], xb_view(at, x)).then_inc(x_in[s], 16)

                        def load_y(k, lag):
                            if k.live(lag):
                                at, s = rows_of(k)(lag), k.slot(lag)
                                if k.has(lag + 4):
                                    sp.wait_ge(xT_done, k.n(lag + 3))
                                    alone(sp, passed)
                                sp.dma_start(yin[:, s, :, :], xb_view(at, ysum)).then_inc(y_in[s], 16)

                        def body(k):
                            if final:
                                if k.peeled and k.c == 0:
                                    load_y(k, 0)
                                    load_y(k, -1)
                                load_y(k, -2)
                                load_x(k, 0)
                            else:
                                if k.peeled and k.c == 0:
                                    for n in range(4):
                                        load_x(k, -n)
                                    load_weights(sp)
                                if k.peeled and 3 <= k.c < 8:
                                    sort.load_edges(k.c - 3)
                                load_x(k, -4)
                        steps(sp, body, sort.sync if sort else None)
                        if sort:
                            sort.load_first_group()
                            sp.wait_ge(s_w2, 16 * 8)
                        if final:
                            wait_stored(sp, stored)

                    if not final:
                        @block.gpsimd
                        def _(pool):
                            def body(k):
                                sort.gpsimd(k, 0)
                                sort.gpsimd(k, 1)
                                if k.live(-3):
                                    s = k.slot(-3)
                                    pool.wait_ge(mv_done, k.n(-4))
                                    alone(pool, passed)
                                    nc.gpsimd.tensor_scalar(ve[:, s, :], mv[:, s, :, 1], EPS, None, ALU.add).then_inc(ve_done, 1)
                                    pool.wait_ge(ve_done, k.n(-4))
                                    nc.gpsimd.tensor_tensor(rstd[:, s, :], ve[:, s, :], neghalf[:, :], ALU.pow).then_inc(rstd_done, 1)
                                sort.gpsimd(k, 2)
                                if k.peeled and k.c >= 0:
                                    clear_stages(pool, k.c)
                            make_constants(pool)
                            clear_stages(pool, -1)
                            for c in (-3, -2, -1):
                                body(Step(0, c, 4, NB))
                            steps(pool, body, sort.gpsimd)
                            sort.finish(pool)

                    @block.vector
                    def _(dve):
                        def stats_of(k, lag):
                            if k.live(lag):
                                s = k.slot(lag)
                                dve.wait_ge(x_in[s], k.uses(lag) * 16)
                                for j in range(TB):
                                    last = nc.vector.bn_stats(stats[:, s, j, :], xin[:, s, j, :])
                                last.then_inc(st_done, 1)

                        def aggregate(k, lag):
                            if k.live(lag):
                                s = k.slot(lag)
                                dve.wait_ge(st_done, k.n(lag - 1))
                                alone(dve, passed)
                                for j in range(TB):
                                    last = nc.vector.bn_aggr(mv[:, s, j, :], stats[:, s, j, :])
                                last.then_inc(mv_done, 1)

                        def normalise(k, lag):
                            if k.live(lag):
                                s = k.slot(lag)
                                dve.wait_ge(rstd_done, k.n(lag - 1))
                                for j in range(TB):
                                    last = nc.vector.tensor_scalar(xn[:, s, j, :], xin[:, s, j, :], mv[:, s, j, 0:1],
                                                                   rstd[:, s, j:j + 1], ALU.subtract, ALU.mult)
                                last.then_inc(norm_done, 1)

                        def body(k):
                            s = k.slot()
                            if not final and k.peeled and k.c == 0:
                                for lag in (0, -1, -2):
                                    stats_of(k, lag)
                                    aggregate(k, lag)
                                normalise(k, 0)
                            if final and k.live():
                                dve.wait_ge(xT_done, k.n(-1))
                                if k.has(4):
                                    dve.wait_ge(s1_done, k.n(3))
                                nc.vector.tensor_copy(hT[:, s, :], psum[0][:, :]).then_inc(hT_done, 1)
                            if not final:
                                beside(k, 0)
                                normalise(k, -1)
                                sort.ranks(k, 0)
                                beside(k, 1)
                                stats_of(k, -3)
                                sort.ranks(k, 1)
                            if k.live(2):
                                q = k.slot(2)
                                dve.wait_ge(b_done, k.n(1))
                                dve.wait_ge(hT_done, k.n(1))
                                if k.has(6):
                                    dve.wait_ge(s3_done, k.n(5))
                                nc.vector.scalar_tensor_tensor(out=h2[:, q, :], in0=psum[2][:, :], scalar=b2_sb[:, m:m + 1],
                                                               in1=hT[:, q, :], op0=ALU.add, op1=ALU.add).then_inc(h2_done, 1)
                            if not final:
                                beside(k, 2)
                                aggregate(k, -3)
                                sort.ranks(k, 2)
                            elif k.live(3):
                                q = k.slot(3)
                                dve.wait_ge(o_done, k.n(2))
                                dve.wait_ge(x_in[q], k.uses(3) * 16)
                                if k.has(7):
                                    dve.wait_ge(stored[q], k.uses(7) * 16)
                                nc.vector.tensor_tensor(rowout[:, q, :, :].rearrange("p t f -> p (t f)"), psum[3][:, :],
                                                        xin[:, q, :, :].rearrange("p t f -> p (t f)"), ALU.add).then_inc(row_done, 1)
                        if sort:
                            derive_constants(dve)
                        beside = sort.vector if sort else None
                        steps(dve, body, beside)

                    @block.scalar
                    def _(act):
                        def relu(k):
                            if k.live():
                                s = k.slot()
                                act.wait_ge(xT_done, k.n(-1))
                                if k.has(4):
                                    act.wait_ge(h2_done, k.n(3))
                                nc.scalar.activation(hT[:, s, :], psum[0][:, :], ACT.Relu).then_inc(hT_done, 1)

                        def silu1(k):
                            if k.live():
                                s = k.slot()
                                act.wait_ge(hT_done, k.n(-1))
                                if k.has(4):
                                    act.wait_ge(a_done, k.n(3))
                                nc.scalar.activation(s1[:, s, :], hT[:, s, :], ACT.Silu).then_inc(s1_done, 1)

                        def silu2(k):
                            if k.live(1):
                                s = k.slot(1)
                                act.wait_ge(a_done, k.n(0))
                                if k.has(5):
                                    act.wait_ge(b_done, k.n(4))
                                nc.scalar.activation(s2[:, s, :], psum[1][:, :], ACT.Silu, bias=b1_sb[:, m:m + 1]).then_inc(s2_done, 1)

                        def silu3(k, lag):
                            if k.live(lag):
                                s = k.slot(lag)
                                act.wait_ge(h2_done, k.n(lag - 1))
                                if k.has(lag + 4):
                                    act.wait_ge(o_done, k.n(lag + 3))
                                nc.scalar.activation(s3[:, s, :], h2[:, s, :], ACT.Silu).then_inc(s3_done, 1)

                        def rows_out(k):
                            if k.live(LAG):
                                s = k.slot(LAG)
                                act.wait_ge(o_done, k.n(LAG - 1))
                                if k.has(LAG + 4):
                                    act.wait_ge(stored[s], k.uses(LAG + 4) * 16)
                                nc.scalar.copy(rowout[:, s, :, :].rearrange("p t f -> p (t f)"), psum[3][:, :]).then_inc(row_done, 1)

                        def body(k):
                            if final:
                                silu1(k)
                                silu2(k)
                                silu3(k, 2)
                                store(act, k)
                            else:
                                rows_out(k)
                                beside(k, 0)
                                silu3(k, 3)
                                beside(k, 1)
                                relu(k)
                                beside(k, 2)
                                silu2(k)
                                store(act, k)
                                silu1(k)
                        beside = sort.scalar if sort else None
                        steps(act, body, beside)

                    @block.tensor
                    def _(pe):
                        def body(k):
                            if k.live():
                                s = k.slot()
                                if final:
                                    pe.wait_ge(y_in[s], k.uses() * 16)
                                else:
                                    pe.wait_ge(norm_done, k.n(-1))
                                if k.has(1):
                                    pe.wait_ge(hT_done, k.n(0))
                                for j in range(TB):
                                    last = nc.tensor.transpose(psum[0][:, j * P:(j + 1) * P], (yin if final else xn)[:, s, j, :], ident[:, :])
                                last.then_inc(xT_done, 1)
                            if k.live(1):
                                s = k.slot(1)
                                pe.wait_ge(s1_done, k.n(0))
                                if k.has(2):
                                    pe.wait_ge(s2_done, k.n(1))
                                nc.tensor.matmul(psum[1][:, :], w1_sb[:, m, :], s1[:, s, :], start=True, stop=True).then_inc(a_done, 1)
                            if sort:
                                beside(k, 0)
                            if k.live(2):
                                s = k.slot(2)
                                pe.wait_ge(s2_done, k.n(1))
                                if k.has(3):
                                    pe.wait_ge(h2_done, k.n(2))
                                nc.tensor.matmul(psum[2][:, :], w2_sb[:, m, :], s2[:, s, :], start=True, stop=True).then_inc(b_done, 1)
                            if sort:
                                beside(k, 1)
                            if k.live(3):
                                s = k.slot(3)
                                pe.wait_ge(s3_done, k.n(2))
                                if k.has(4):
                                    pe.wait_ge(row_done, k.n(3))
                                for j in range(TB):
                                    last = nc.tensor.matmul(psum[3][:, j * P:(j + 1) * P], s3[:, s, j * P:(j + 1) * P], wo_sb[:, m, :],
                                                            start=True, stop=True)
                                last.then_inc(o_done, 1)
                            if sort:
                                beside(k, 2)
                        if sort:
                            pe.wait_ge(s_dve, 3)
                            pe.wait_ge(s_w, 16 * 5)
                        beside = sort.tensor if sort else None
                        steps(pe, body, beside)
            return stored

        node_stored = node_phase(False, Sort())
        own.close()
        edge_phase(nc, locals())
        node_phase(True)


def edge_phase(nc, env):
    fp32, i32 = mybir.dt.float32, mybir.dt.int32
    ALU = mybir.AluOpType
    ACT = mybir.ActivationFunctionType
    P, F, TB, V, R, G, KT, W, BLOCK, EPS = (env[n] for n in ("P", "F", "TB", "V", "R", "G", "KT", "W", "BLOCK", "EPS"))
    x, by_src, ysum, psum, sb = (env[n] for n in ("x", "by_src", "ysum", "psum", "sb"))
    ident, unit, trash, is_real, neghalf, zeros = (
        env[n] for n in ("ident", "unit", "trash", "is_real", "neghalf", "zeros"))
    w1_sb, w2_sb, wo_sb, b1_sb, b2_sb, wr_sb, wpp_sb, wpd_sb = (
        env[n] for n in ("w1_sb", "w2_sb", "wo_sb", "b1_sb", "b2_sb", "wr_sb", "wpp_sb", "wpd_sb"))
    wait_stored, node_stored = env["wait_stored"], env["node_stored"]
    er, nxt, rows_in, x_in, unit_done, U = (env[n] for n in ("er", "nxt", "rows_in", "gathered", "unit_done", "U"))
    xg, xn, stats, mv, ve, rstd, hT, s1, s2, h2, s3, urow = (
        env[n] for n in ("yin", "xn", "stats", "mv", "ve", "rstd", "hT", "s1", "s2", "h2", "s3", "rowout"))
    MLP = (2, 3, 1)
    C_ONE, C_P, C_D, C_RBF_B = (env[n] for n in ("C_ONE", "C_P", "C_D", "C_RBF_B"))
    srcf = sb("srcf", [P, U, TB])
    nxtf = sb("nxtf", [P, U, TB])
    ends = sb("ends", [P, U, TB])
    row_f = sb("row_f", [P, U, TB])
    row_i = sb("row_i", [P, U, TB], i32)
    eT = sb("eT", [KT, U, BLOCK])
    gate = sb("gate", [P, 3, BLOCK])
    mT = sb("mT", [P, U, 2, BLOCK])
    msg = sb("msg", [P, U, TB, F])
    AB = sb("AB", [P, 2, 4, F])
    same = sb("same", [P, 2, P])
    gram = sb("gram", [P, 2, 2, P])
    last_w = sb("last_w", [P, 2, C_RBF_B])
    prod = sb("prod", [P, 2, 2, F])
    allsum = sb("allsum", [P, 2, 2, F])

    HT_AT_G, BANK_A, BANK_B, BANK_O, BANK_AB, BANK_SEG, BANK_C, BANK_TU = psum
    SRC_T, GRAM, S_CARRY = BANK_SEG[:, 0:P], BANK_SEG[:, P:3 * P], BANK_C[0:V, 0:F]
    BANK_T, BANK_U = BANK_TU[:, 0:2 * F], BANK_TU[:, 3 * F:4 * F]

    with ExitStack() as own:
        def sem(nm):
            return own.enter_context(nc.semaphore("e_" + nm))
        added = [sem(f"added{i}") for i in range(TB)]
        srcf_done, idx_a, idx_b, row_done = (sem(s) for s in ("srcf_done", "offsets_made", "ends_masked", "rows_done"))
        st_done, mv_done, ve_done, rstd_done, norm_done = (sem(s) for s in ("stats_done", "meanvar_done", "vareps_done", "rstd_done", "norm_done"))
        xT_done, hT_done, s1_done, eT_ps, eT_done = (sem(s) for s in ("xT_done", "hT_done", "s1_done", "eT_in_psum", "eT_done"))
        a_done, s2_done, b_done, h2_done, s3_done, g_ps, gate_done, o_done, msg_done = (
            sem(s) for s in ("a_done", "s2_done", "b_done", "h2_done", "s3_done", "gate_in_psum", "gate_done", "o_done", "msg_done"))
        gram3_ps, seg_ps, ab_ps, ab_done, same_done, gram_done, lastw_done, c_done, ms_done = (
            sem(s) for s in ("gram3_in_psum", "seg_in_psum", "ab_in_psum", "ab_done", "same_done", "gram_done", "last_weights_done", "carry_done", "sums_carried"))
        t_done, prod_done, sum1_done, sum_done, u_ps, u_done = (
            sem(s) for s in ("t_done", "prod_done", "sum1_done", "sum_done", "u_in_psum", "u_done"))

        passed = sem("waits_passed")

        def steps(eng, body):
            run_steps(eng, body, U, G, U + 1, 2, 1)

        def nm(k, lag, m, plus=0):
            return k.n(lag) * 3 + (m + plus)

        def nt(k, j, plus=0):
            return k.n(1) * TB + (j + plus)

        def first_tile(k, j, back):
            return k.peeled and (k.c - 1) * TB + j - back < 0

        def previous(k, j):
            return k.live(1 if j else 2)

        with nc.Block() as block:
            @block.sync
            def _(sp):
                def load(k, lag):
                    if not k.live(lag):
                        return
                    s = k.slot(lag)
                    if k.has(lag + U):
                        sp.wait_ge(lastw_done, k.n(lag + U - 1) * TB)
                        alone(sp, passed)
                        sp.wait_ge(row_done, k.n(lag + U - 1))
                        alone(sp, passed)
                        sp.wait_ge(x_in[s], k.uses(lag + U) * 64)
                        alone(sp, passed)
                    start = k.n(lag) * (TB * R)
                    with nc.allow_non_contiguous_dma(reason="one word of each row"):
                        load_group(sp, by_src, er, nxt, s, start, V, R, TB, rows_in[s])

                def body(k):
                    load(k, -1)
                steps(sp, body)

            @block.gpsimd
            def _(pool):
                def carry_rows(k, lag):
                    if not k.live(lag):
                        return
                    s = k.slot(lag)
                    pool.wait_ge(rows_in[s], k.uses(lag) * 48)
                    alone(pool, passed)
                    nc.gpsimd.tensor_copy(er[0:V, s, :, 2:W], unit[:, :, :]).then_inc(unit_done, 1)

                def gather(k, lag, tiles):
                    if not k.live(lag):
                        return
                    s = k.slot(lag)
                    if k.has(lag + U) and tiles[0] == 0:
                        pool.wait_ge(norm_done, k.n(lag + U - 1))
                        alone(pool, passed)
                    for j in tiles:
                        gather_tile(nc.gpsimd, x, xg, er, s, j, x_in[s])

                def scale(k, lag):
                    if k.live(lag):
                        s = k.slot(lag)
                        pool.wait_ge(mv_done, k.n(lag - 1))
                        alone(pool, passed)
                        nc.gpsimd.tensor_scalar(ve[:, s, :], mv[:, s, :, 1], EPS, None, ALU.add).then_inc(ve_done, 1)
                        pool.wait_ge(ve_done, k.n(lag - 1))
                        nc.gpsimd.tensor_tensor(rstd[:, s, :], ve[:, s, :], neghalf[:, :], ALU.pow).then_inc(rstd_done, 1)

                def add_row(k, j):
                    if previous(k, j):
                        b, s = (j - 1) % TB, k.slot(1 if j else 2)
                        pool.wait_ge(u_done, nt(k, j))
                        if not first_tile(k, j, 2):
                            pool.wait_ge(added[(j - 2) % TB], (k.n(0) if j > 1 else k.n(1)) * 16)
                        alone(pool, passed)
                        nc.gpsimd.indirect_dma_start(
                            out=ysum, out_offset=bass.IndirectOffsetOnAxis(ap=row_i[:, s, b:b + 1], axis=0),
                            in_=urow[:, b, 0, :], in_offset=None, compute_op=ALU.add).then_inc(added[b], 16)

                def all_sums(k, j):
                    if k.live(1):
                        s = k.slot(1)
                        pool.wait_ge(prod_done, nt(k, j, 1))
                        if not first_tile(k, j, 2):
                            pool.wait_ge(u_ps, nt(k, j, -1))
                        nc.gpsimd.tensor_tensor(allsum[:, j % 2, 0, :], prod[:, j % 2, 0, :], prod[:, j % 2, 1, :], ALU.add).then_inc(sum1_done, 1)
                        pool.wait_ge(sum1_done, nt(k, j, 1))
                        pool.wait_ge(ms_done, nt(k, j, 1))
                        nc.gpsimd.tensor_tensor(allsum[:, j % 2, 1, :], allsum[:, j % 2, 0, :], msg[:, s, j, :], ALU.add).then_inc(sum_done, 1)

                def body(k):
                    if k.peeled and k.c == 0:
                        scale(k, 0)
                        wait_stored(pool, node_stored)
                    carry_rows(k, -1)
                    gather(k, -1, (0, 1))
                    add_row(k, 0)
                    all_sums(k, 0)
                    gather(k, -1, (2, 3))
                    add_row(k, 1)
                    all_sums(k, 1)
                    scale(k, -1)
                    add_row(k, 2)
                    all_sums(k, 2)
                    add_row(k, 3)
                    all_sums(k, 3)
                steps(pool, body)
                for j in range(TB):
                    pool.wait_ge(added[j], 16 * G)

            @block.vector
            def _(dve):
                def indices(k, lag):
                    if not k.live(lag):
                        return
                    s = k.slot(lag)
                    n = k.n(lag - 1)
                    dve.wait_ge(rows_in[s], k.uses(lag) * 48)
                    if k.has(lag + U):
                        dve.wait_ge(seg_ps, k.n(lag + U - 1) * TB)
                        dve.wait_ge(added[TB - 1], k.n(lag + U - 1) * 16)
                    nc.vector.tensor_copy(srcf[:, s, :], er[:, s, :, 0].bitcast(i32))
                    nc.vector.tensor_copy(nxtf[:, s, :], nxt[:, s, :]).then_inc(srcf_done, 1)
                    dve.wait_ge(srcf_done, n)
                    nc.vector.tensor_tensor(ends[:, s, :], srcf[:, s, :], nxtf[:, s, :], ALU.not_equal)
                    nc.vector.tensor_scalar(row_f[:, s, :], srcf[:, s, :], trash[:, 0:1], is_real[:, 0:1], ALU.subtract, ALU.mult).then_inc(idx_a, 1)
                    dve.wait_ge(idx_a, n)
                    nc.vector.tensor_tensor(nxtf[:, s, :], row_f[:, s, :], ends[:, s, :], ALU.mult).then_inc(idx_b, 1)
                    dve.wait_ge(idx_b, n)
                    nc.vector.tensor_scalar(row_i[:, s, :], nxtf[:, s, :], trash[:, 0:1], None, ALU.add).then_inc(row_done, 1)

                def stats_of(k, lag):
                    if k.live(lag):
                        s = k.slot(lag)
                        dve.wait_ge(x_in[s], k.uses(lag) * 64)
                        for j in range(TB):
                            last = nc.vector.bn_stats(stats[:, s, j, :], xg[:, s, j, :])
                        last.then_inc(st_done, 1)
                        dve.wait_ge(st_done, k.n(lag - 1))
                        alone(dve, passed)
                        for j in range(TB):
                            last = nc.vector.bn_aggr(mv[:, s, j, :], stats[:, s, j, :])
                        last.then_inc(mv_done, 1)

                def normalise(k, lag):
                    if k.live(lag):
                        s = k.slot(lag)
                        dve.wait_ge(rstd_done, k.n(lag - 1))
                        if k.has(lag + U):
                            dve.wait_ge(xT_done, k.n(lag + U - 1))
                        for j in range(TB):
                            last = nc.vector.tensor_scalar(xn[:, s, j, :], xg[:, s, j, :], mv[:, s, j, 0:1],
                                                           rstd[:, s, j:j + 1], ALU.subtract, ALU.mult)
                        last.then_inc(norm_done, 1)

                def residual(k, m):
                    if k.live():
                        dve.wait_ge(b_done, nm(k, 0, m, 1))
                        if k.has(1):
                            dve.wait_ge(s3_done, nm(k, 1, m, 1))
                        nc.vector.scalar_tensor_tensor(out=h2[:, m, :], in0=BANK_B[:, :], scalar=b2_sb[:, MLP[m]:MLP[m] + 1],
                                                       in1=hT[:, k.slot(), :], op0=ALU.add, op1=ALU.add).then_inc(h2_done, 1)

                def message(k, m):
                    if k.live():
                        s = k.slot()
                        dve.wait_ge(o_done, nm(k, 0, m, 1))
                        dve.wait_ge(gate_done, nm(k, 0, m, 1))
                        if k.has(U):
                            dve.wait_ge(ab_ps if m < 2 else sum_done, k.n(U - 1) * TB)
                            if m == 2:
                                dve.wait_ge(c_done, k.n(U - 1) * TB)
                        dest = mT[:, s, m, :] if m < 2 else msg[:, s, :, :].rearrange("p t f -> p (t f)")
                        nc.vector.tensor_tensor(dest, BANK_O[:, :], gate[:, m, :], ALU.mult).then_inc(msg_done, 1)

                def seg_masks(k, j):
                    if k.live(1):
                        s, q = k.slot(1), j % 2
                        dve.wait_ge(seg_ps, nt(k, j, 1))
                        if not first_tile(k, j, 2):
                            dve.wait_ge(u_ps, nt(k, j, -1))
                            dve.wait_ge(t_done, nt(k, j, -1))
                            dve.wait_ge(c_done, nt(k, j, -1))
                        nc.vector.tensor_scalar(same[:, q, :], SRC_T, srcf[:, s, j:j + 1], None, ALU.is_equal).then_inc(same_done, 1)
                        dve.wait_ge(same_done, nt(k, j, 1))
                        nc.vector.tensor_tensor(gram[:, q, :, :], GRAM.rearrange("p (a b) -> p a b", a=2),
                                                same[:, q, :].unsqueeze(1).to_broadcast([P, 2, P]), ALU.mult).then_inc(gram_done, 1)
                        nc.vector.tensor_scalar(last_w[:, q, :], er[:, s, j, 2:2 + C_RBF_B], same[:, q, P - 1:P], None, ALU.mult).then_inc(lastw_done, 1)

                def seg_carry(k, j):
                    if k.live(1):
                        s = k.slot(1)
                        dve.wait_ge(msg_done, k.n(0) * 3)
                        if first_tile(k, j, 1):
                            nc.vector.tensor_copy(msg[0:V, s, j, :], zeros[0:V, 0:F]).then_inc(ms_done, 1)
                        else:
                            dve.wait_ge(c_done, nt(k, j, 0))
                            nc.vector.tensor_copy(msg[0:V, s, j, :], S_CARRY).then_inc(ms_done, 1)

                def seg_prod(k, j):
                    if k.live(1):
                        q = j % 2
                        dve.wait_ge(t_done, nt(k, j, 1))
                        dve.wait_ge(ab_done, nt(k, j, 1))
                        if not first_tile(k, j, 2):
                            dve.wait_ge(sum1_done, nt(k, j, -1))
                        nc.vector.tensor_tensor(prod[:, q, :, :], BANK_T.rearrange("p (a b) -> p a b", a=2),
                                                AB[:, q, :, :].rearrange("p (a b) f -> p a b f", b=2)[:, :, 0, :], ALU.mult).then_inc(prod_done, 1)

                def rectify(k, lag):
                    if k.live(lag):
                        dve.wait_ge(xT_done, k.n(lag - 1))
                        if k.has(lag + U):
                            dve.wait_ge(s1_done, k.n(lag + U - 1))
                        nc.vector.tensor_scalar_max(hT[:, k.slot(lag), :], HT_AT_G[:, :], 0.0).then_inc(hT_done, 1)

                def body(k):
                    if k.peeled and k.c == 0:
                        indices(k, 0)
                        stats_of(k, 0)
                        normalise(k, 0)
                        rectify(k, 0)
                    seg_masks(k, 0)
                    seg_carry(k, 0)
                    seg_prod(k, 0)
                    indices(k, -1)
                    seg_masks(k, 1)
                    seg_carry(k, 1)
                    residual(k, 0)
                    seg_prod(k, 1)
                    stats_of(k, -1)
                    seg_masks(k, 2)
                    seg_carry(k, 2)
                    residual(k, 1)
                    message(k, 0)
                    seg_prod(k, 2)
                    normalise(k, -1)
                    seg_masks(k, 3)
                    seg_carry(k, 3)
                    residual(k, 2)
                    message(k, 1)
                    rectify(k, -1)
                    seg_prod(k, 3)
                    message(k, 2)
                steps(dve, body)

            @block.scalar
            def _(act):
                def silu1(k, lag):
                    if k.live(lag):
                        act.wait_ge(hT_done, k.n(lag - 1))
                        if k.has(lag + U):
                            act.wait_ge(a_done, nm(k, lag + U, 2, 1))
                        nc.scalar.activation(s1[:, k.slot(lag), :], hT[:, k.slot(lag), :], ACT.Silu).then_inc(s1_done, 1)

                def silu2(k, m):
                    if k.live():
                        act.wait_ge(a_done, nm(k, 0, m, 1))
                        if k.has(1):
                            act.wait_ge(b_done, nm(k, 1, m, 1))
                        nc.scalar.activation(s2[:, m, :], BANK_A[:, :], ACT.Silu, bias=b1_sb[:, MLP[m]:MLP[m] + 1]).then_inc(s2_done, 1)

                def silu3(k, m):
                    if k.live():
                        act.wait_ge(h2_done, nm(k, 0, m, 1))
                        if k.has(1):
                            act.wait_ge(o_done, nm(k, 1, m, 1))
                        nc.scalar.activation(s3[:, m, :], h2[:, m, :], ACT.Silu).then_inc(s3_done, 1)

                def edges_T(k, lag):
                    if k.live(lag):
                        act.wait_ge(eT_ps, k.n(lag - 1))
                        if k.has(lag + U):
                            act.wait_ge(seg_ps, k.n(lag + U - 1) * TB)
                        nc.scalar.copy(eT[:, k.slot(lag), :], HT_AT_G[0:KT, :]).then_inc(eT_done, 1)

                def gates(k, m):
                    if k.live():
                        act.wait_ge(g_ps, nm(k, 0, m, 1))
                        if k.has(1):
                            act.wait_ge(msg_done, nm(k, 1, m, 1))
                        nc.scalar.copy(gate[:, m, :], HT_AT_G[:, :]).then_inc(gate_done, 1)

                def halves(k, j):
                    if k.live(1):
                        q = j % 2
                        act.wait_ge(ab_ps, nt(k, j, 1))
                        if not first_tile(k, j, 2):
                            act.wait_ge(c_done, nt(k, j, -1))
                            act.wait_ge(t_done, nt(k, j, -1))
                            act.wait_ge(prod_done, nt(k, j, -1))
                        nc.scalar.copy(AB[:, q, :, :].rearrange("p a f -> p (a f)"), BANK_AB[:, :]).then_inc(ab_done, 1)

                def sums_out(k, j):
                    if previous(k, j):
                        b = (j - 1) % TB
                        act.wait_ge(u_ps, nt(k, j))
                        if not first_tile(k, j, TB + 1):
                            act.wait_ge(added[b], (k.n(1) if j else k.n(2)) * 16)
                        nc.scalar.copy(urow[:, b, 0, :], BANK_U).then_inc(u_done, 1)

                def body(k):
                    if k.peeled and k.c == 0:
                        silu1(k, 0)
                        edges_T(k, 0)
                    silu2(k, 0)
                    halves(k, 0)
                    sums_out(k, 0)
                    gates(k, 0)
                    silu2(k, 1)
                    halves(k, 1)
                    sums_out(k, 1)
                    silu3(k, 0)
                    gates(k, 1)
                    silu2(k, 2)
                    halves(k, 2)
                    sums_out(k, 2)
                    silu3(k, 1)
                    gates(k, 2)
                    halves(k, 3)
                    sums_out(k, 3)
                    silu3(k, 2)
                    silu1(k, -1)
                    edges_T(k, -1)
                steps(act, body)

            @block.tensor
            def _(pe):
                def rows_T(k, lag):
                    if k.live(lag):
                        pe.wait_ge(norm_done, k.n(lag - 1))
                        if k.has(lag + 1):
                            pe.wait_ge(gate_done, nm(k, lag + 1, 2, 1))
                        for j in range(TB):
                            last = nc.tensor.transpose(HT_AT_G[:, j * P:(j + 1) * P], xn[:, k.slot(lag), j, :], ident[:, :])
                        last.then_inc(xT_done, 1)

                def edges_T(k, lag):
                    if k.live(lag):
                        s = k.slot(lag)
                        pe.wait_ge(unit_done, k.n(lag - 1))
                        pe.wait_ge(rows_in[s], k.uses(lag) * 48)
                        pe.wait_ge(hT_done, k.n(lag - 1))
                        alone(pe, passed)
                        for j in range(TB):
                            last = nc.tensor.transpose(HT_AT_G[0:KT, j * P:(j + 1) * P], er[:, s, j, 2:W], ident[:, :])
                        last.then_inc(eT_ps, 1)

                def up(k, m):
                    if k.live():
                        pe.wait_ge(s1_done, k.n(-1))
                        if m or k.has(1):
                            pe.wait_ge(s2_done, nm(k, 0, m, 0))
                        nc.tensor.matmul(BANK_A[:, :], w1_sb[:, MLP[m], :], s1[:, k.slot(), :], start=True, stop=True).then_inc(a_done, 1)

                def down(k, m):
                    if k.live():
                        pe.wait_ge(s2_done, nm(k, 0, m, 1))
                        if m or k.has(1):
                            pe.wait_ge(h2_done, nm(k, 0, m, 0))
                        nc.tensor.matmul(BANK_B[:, :], w2_sb[:, MLP[m], :], s2[:, m, :], start=True, stop=True).then_inc(b_done, 1)

                def gates(k, m):
                    if k.live():
                        pe.wait_ge(eT_done, k.n(-1))
                        if m:
                            pe.wait_ge(gate_done, nm(k, 0, m, 0))
                        if m < 2:
                            last = nc.tensor.matmul(HT_AT_G[:, :], wr_sb[:, m, :], eT[:, k.slot(), :], start=True, stop=True)
                        else:
                            for j in range(TB):
                                last = nc.tensor.matmul(HT_AT_G[:, j * P:(j + 1) * P], eT[:, k.slot(), j * P:(j + 1) * P], wr_sb[:, m, :], start=True, stop=True)
                        last.then_inc(g_ps, 1)

                def outp(k, m):
                    if k.live():
                        pe.wait_ge(s3_done, nm(k, 0, m, 1))
                        if m or k.has(1):
                            pe.wait_ge(msg_done, nm(k, 0, m, 0))
                        if m < 2:
                            last = nc.tensor.matmul(BANK_O[:, :], wo_sb[:, MLP[m], :], s3[:, m, :], start=True, stop=True)
                        else:
                            for j in range(TB):
                                last = nc.tensor.matmul(BANK_O[:, j * P:(j + 1) * P], s3[:, m, j * P:(j + 1) * P], wo_sb[:, MLP[m], :], start=True, stop=True)
                        last.then_inc(o_done, 1)

                def seg(k, j):
                    if k.live(1):
                        s, cols = k.slot(1), slice(j * P, (j + 1) * P)
                        pe.wait_ge(row_done, k.n(0))
                        if not first_tile(k, j, 1):
                            pe.wait_ge(gram_done, nt(k, j))
                        nc.tensor.matmul(GRAM[:, 0:P], eT[C_P:C_P + V, s, cols], eT[C_P:C_P + V, s, cols], start=True, stop=True).then_inc(gram3_ps, 1)
                        nc.tensor.transpose(SRC_T, srcf[:, s, j:j + 1].to_broadcast([P, P]), ident[:, :])
                        pe.wait_ge(msg_done, nm(k, 1, 1, 1))
                        if not first_tile(k, j, 1):
                            pe.wait_ge(ab_done, nt(k, j, 0))
                        nc.tensor.matmul(BANK_AB[:, 0:2 * F], mT[:, s, 0, cols], wpp_sb[:, :], start=True, stop=True)
                        pe.wait_ge(gram3_ps, nt(k, j, 1))
                        nc.tensor.matmul(GRAM[:, P:2 * P], eT[C_D:C_D + V, s, cols], eT[C_D:C_D + V, s, cols], start=True, stop=True).then_inc(seg_ps, 1)
                        last = nc.tensor.matmul(BANK_AB[:, 2 * F:4 * F], mT[:, s, 1, cols], wpd_sb[:, :], start=True, stop=True)
                        if first_tile(k, j, 1):
                            last.then_inc(ab_ps, 1)

                def carry(k, j):
                    if k.live(1) and not first_tile(k, j, 1):
                        b, s, q = (j - 1) % TB, k.slot(1 if j else 2), (j - 1) % 2
                        pe.wait_ge(lastw_done, nt(k, j))
                        pe.wait_ge(ab_done, nt(k, j))
                        pe.wait_ge(ms_done, nt(k, j))
                        flat = AB[:, q, :, :].rearrange("p a f -> p (a f)")
                        nc.tensor.matmul(BANK_AB[0:V, 0:2 * F], last_w[:, q, C_P:C_P + V], flat[:, 0:2 * F],
                                         start=False, stop=True, skip_group_check=True)
                        nc.tensor.matmul(BANK_AB[0:V, 2 * F:4 * F], last_w[:, q, C_D:C_D + V], flat[:, 2 * F:4 * F],
                                         start=False, stop=True, skip_group_check=True).then_inc(ab_ps, 1)
                        nc.tensor.matmul(S_CARRY, last_w[:, q, C_ONE:C_ONE + V], msg[:, s, b, :], start=True, stop=True).then_inc(c_done, 1)

                def inner(k, j):
                    if k.live(1):
                        q = j % 2
                        pe.wait_ge(gram_done, nt(k, j, 1))
                        pe.wait_ge(ab_done, nt(k, j, 1))
                        if not first_tile(k, j, 1):
                            pe.wait_ge(u_done, nt(k, j))
                        nc.tensor.matmul(BANK_T[:, 0:F], gram[:, q, 0, :], AB[:, q, 1, :], start=True, stop=True)
                        nc.tensor.matmul(BANK_T[:, F:2 * F], gram[:, q, 1, :], AB[:, q, 3, :], start=True, stop=True).then_inc(t_done, 1)

                def sums(k, j):
                    if previous(k, j):
                        q = (j - 1) % 2
                        pe.wait_ge(sum_done, nt(k, j))
                        nc.tensor.matmul(BANK_U, same[:, q, :], allsum[:, q, 1, :], start=True, stop=True).then_inc(u_ps, 1)

                def body(k):
                    if k.peeled and k.c == 0:
                        rows_T(k, 0)
                        edges_T(k, 0)
                    up(k, 0)
                    seg(k, 0)
                    carry(k, 0)
                    sums(k, 0)
                    gates(k, 0)
                    inner(k, 0)
                    up(k, 1)
                    seg(k, 1)
                    carry(k, 1)
                    sums(k, 1)
                    down(k, 0)
                    gates(k, 1)
                    inner(k, 1)
                    up(k, 2)
                    seg(k, 2)
                    carry(k, 2)
                    sums(k, 2)
                    down(k, 1)
                    outp(k, 0)
                    inner(k, 2)
                    gates(k, 2)
                    seg(k, 3)
                    carry(k, 3)
                    sums(k, 3)
                    down(k, 2)
                    outp(k, 1)
                    rows_T(k, -1)
                    inner(k, 3)
                    outp(k, 2)
                    edges_T(k, -1)
                steps(pe, body)


_PRE = "L0_gnn_"
_INS = ["x", "src", "dst", "edge_attr_3", "edge_attr_32", "edge_attr_5"] + [
    _PRE + n for n in ("w_rs", "w_rp", "w_rd", "w_pp", "w_pd", "res_w1", "res_b1", "res_w2", "res_b2", "res_wout")]


def kernel(**inputs):
    import numpy as _np
    import concourse.bacc as _bacc
    from concourse import mybir as _mybir
    from concourse.bass_utils import run_bass_kernel_spmd as _run

    nc = _bacc.Bacc("TRN2", target_bir_lowering=False, num_devices=1)
    arrays, args = {}, []
    for name in _INS:
        a = _np.ascontiguousarray(inputs[name])
        arrays[f"in_{name}_dram"] = a
        args.append(nc.dram_tensor(f"in_{name}_dram", a.shape, _mybir.dt.from_np(a.dtype), kind="ExternalInput").ap())
    out = nc.dram_tensor("out_0_dram", inputs["x"].shape, _mybir.dt.float32, kind="ExternalOutput").ap()
    gnn_kernel(nc, *args, out)
    r = _run(nc, [arrays], core_ids=[0])
    return r.results[0]["out_0_dram"]
```
